# Optimizing a Trainium2 kernel written in Bass

```python
import numpy as np
import jax
import jax.numpy as jnp

def _softmax(x, axis=-1):
    return jax.nn.softmax(x, axis=axis)

def _gelu(x):
    return jax.nn.gelu(x, approximate=True)

def _silu(x):
    return jax.nn.silu(x)

def _sigmoid(x):
    return jax.nn.sigmoid(x)

def _layernorm(x, axis=-1, eps=1e-05):
    m = jnp.mean(x, axis=axis, keepdims=True)
    v = jnp.var(x, axis=axis, keepdims=True)
    return (x - m) / jnp.sqrt(v + eps)

def _scatter_add(tgt, idx, src, axis=0):
    return tgt.at[idx].add(src)

def _segment_sum(src, seg, n):
    return jax.ops.segment_sum(src, seg, n)
kernel_name = 'mk_recurrent_d1_jaxref_r8_30a88d'

def setup_inputs(seed: int=0):
    np.random.seed(seed)
    _w = jnp.asarray

    def _L0_attn_setup():
        import jax, jax.numpy as jnp
        import numpy as np
        D_MODEL = 128
        D_STATE = 128
        D_CONV = 4
        EXPAND = 2
        D_INNER = EXPAND * D_MODEL
        HEADDIM = 64
        NHEADS = D_INNER // HEADDIM
        NGROUPS = 1
        CONV_DIM = D_INNER + 2 * NGROUPS * D_STATE
        D_IN_PROJ = 2 * D_INNER + 2 * NGROUPS * D_STATE + NHEADS
        BATCH, SEQLEN = (2, 256)

        def _mamba2(u, Wi, conv_w, conv_b, dt_bias, A_log, D, norm_w, Wo):
            b, L, _ = u.shape
            zxbcdt = u @ Wi.T
            z = zxbcdt[..., :D_INNER]
            xBC = zxbcdt[..., D_INNER:D_INNER + CONV_DIM]
            dt = zxbcdt[..., D_INNER + CONV_DIM:]
            xBC_t = jnp.moveaxis(xBC, 1, 2)
            xBC_t = jnp.pad(xBC_t, ((0, 0), (0, 0), (D_CONV - 1, 0)))
            conv = jax.lax.conv_general_dilated(xBC_t, conv_w, (1,), 'VALID', feature_group_count=CONV_DIM, dimension_numbers=('NCH', 'OIH', 'NCH'))
            xBC = jax.nn.silu(jnp.moveaxis(conv, 1, 2) + conv_b)
            x = xBC[..., :D_INNER].reshape(b, L, NHEADS, HEADDIM)
            Bm = xBC[..., D_INNER:D_INNER + NGROUPS * D_STATE].reshape(b, L, D_STATE)
            Cm = xBC[..., D_INNER + NGROUPS * D_STATE:].reshape(b, L, D_STATE)
            dt = jax.nn.softplus(dt + dt_bias)
            A = -jnp.exp(A_log)

            def step(h, inp):
                x_t, B_t, C_t, dt_t = inp
                dA = jnp.exp(dt_t * A)
                h = h * dA[..., None, None] + (dt_t[..., None] * x_t)[..., None] * B_t[:, None, None, :]
                y_t = jnp.einsum('bhpn,bn->bhp', h, C_t)
                return (h, y_t)
            h0 = jnp.zeros((b, NHEADS, HEADDIM, D_STATE), u.dtype)
            xs = (jnp.moveaxis(x, 1, 0), jnp.moveaxis(Bm, 1, 0), jnp.moveaxis(Cm, 1, 0), jnp.moveaxis(dt, 1, 0))
            _, ys = jax.lax.scan(step, h0, xs)
            y = jnp.moveaxis(ys, 0, 1) + D[None, None, :, None] * x
            y = y.reshape(b, L, D_INNER)
            y = y * jax.nn.silu(z)
            y = y * jax.lax.rsqrt(jnp.mean(y * y, axis=-1, keepdims=True) + 1e-05) * norm_w
            return y @ Wo.T
        key = jax.random.key(seed)
        ks = jax.random.split(key, 21)

        def lin(k, o, i):
            return jax.random.normal(k, (o, i), jnp.float32) / np.sqrt(i).astype(np.float32)
        d = {'u': jax.random.normal(ks[0], (BATCH, SEQLEN, D_MODEL), jnp.float32)}
        for i, sfx in enumerate(['f', 'b']):
            b0 = 1 + i * 10
            d[f'Wi_{sfx}'] = lin(ks[b0], D_IN_PROJ, D_MODEL)
            d[f'conv_w_{sfx}'] = jax.random.normal(ks[b0 + 1], (CONV_DIM, 1, D_CONV), jnp.float32) / np.sqrt(D_CONV).astype(np.float32)
            d[f'conv_b_{sfx}'] = jnp.zeros((CONV_DIM,), jnp.float32)
            dt = jnp.exp(jax.random.uniform(ks[b0 + 2], (NHEADS,), jnp.float32) * (np.log(0.1) - np.log(0.001)) + np.log(0.001))
            d[f'dt_bias_{sfx}'] = dt + jnp.log(-jnp.expm1(-dt))
            d[f'A_log_{sfx}'] = jnp.log(jax.random.uniform(ks[b0 + 3], (NHEADS,), jnp.float32, minval=1.0, maxval=16.0))
            d[f'D_{sfx}'] = jnp.ones((NHEADS,), jnp.float32)
            d[f'norm_w_{sfx}'] = jnp.ones((D_INNER,), jnp.float32)
            d[f'Wo_{sfx}'] = lin(ks[b0 + 4], D_MODEL, D_INNER)
        return d
    _L0_attn_in = _L0_attn_setup()

    def _L0_ffn_setup():
        import jax, jax.numpy as jnp
        import numpy as np
        NUM_EXPERTS = 160
        TOP_K = 8
        ROUTED_SCALE = 2.5
        HIDDEN = 128
        INTER = 64
        key = jax.random.key(seed)
        ks = jax.random.split(key, 7)
        B, S = (1, 256)
        return {'hidden_states': jax.random.normal(ks[0], (B, S, HIDDEN), dtype=jnp.float32), 'router_w': jax.random.normal(ks[1], (NUM_EXPERTS, HIDDEN), dtype=jnp.float32) * 0.02, 'expert_bias': jnp.zeros((NUM_EXPERTS,), dtype=jnp.float32), 'w_gate': jax.random.normal(ks[2], (NUM_EXPERTS, INTER, HIDDEN), dtype=jnp.float32) * 0.02, 'w_down': jax.random.normal(ks[3], (NUM_EXPERTS, HIDDEN, INTER), dtype=jnp.float32) * 0.02, 'w_gate_shared': jax.random.normal(ks[4], (INTER, HIDDEN), dtype=jnp.float32) * 0.02, 'w_down_shared': jax.random.normal(ks[5], (HIDDEN, INTER), dtype=jnp.float32) * 0.02}
    _L0_ffn_in = _L0_ffn_setup()
    _d = {'L0_attn_u': _L0_attn_in['u'], 'L0_attn_Wi_f': _L0_attn_in['Wi_f'], 'L0_attn_conv_w_f': _L0_attn_in['conv_w_f'], 'L0_attn_conv_b_f': _L0_attn_in['conv_b_f'], 'L0_attn_dt_bias_f': _L0_attn_in['dt_bias_f'], 'L0_attn_A_log_f': _L0_attn_in['A_log_f'], 'L0_attn_D_f': _L0_attn_in['D_f'], 'L0_attn_norm_w_f': _L0_attn_in['norm_w_f'], 'L0_attn_Wo_f': _L0_attn_in['Wo_f'], 'L0_attn_Wi_b': _L0_attn_in['Wi_b'], 'L0_attn_conv_w_b': _L0_attn_in['conv_w_b'], 'L0_attn_conv_b_b': _L0_attn_in['conv_b_b'], 'L0_attn_dt_bias_b': _L0_attn_in['dt_bias_b'], 'L0_attn_A_log_b': _L0_attn_in['A_log_b'], 'L0_attn_D_b': _L0_attn_in['D_b'], 'L0_attn_norm_w_b': _L0_attn_in['norm_w_b'], 'L0_attn_Wo_b': _L0_attn_in['Wo_b'], 'L0_ffn_router_w': _L0_ffn_in['router_w'], 'L0_ffn_expert_bias': _L0_ffn_in['expert_bias'], 'L0_ffn_w_gate': _L0_ffn_in['w_gate'], 'L0_ffn_w_down': _L0_ffn_in['w_down'], 'L0_ffn_w_gate_shared': _L0_ffn_in['w_gate_shared'], 'L0_ffn_w_down_shared': _L0_ffn_in['w_down_shared']}
    _x0 = _d['L0_attn_u']
    _d['L0_attn_u'] = jax.random.normal(jax.random.fold_in(jax.random.key(seed), 1), (8, 1024, 128), dtype=_x0.dtype)
    del _x0
    return _d

def reference(L0_attn_u, L0_attn_Wi_f, L0_attn_conv_w_f, L0_attn_conv_b_f, L0_attn_dt_bias_f, L0_attn_A_log_f, L0_attn_D_f, L0_attn_norm_w_f, L0_attn_Wo_f, L0_attn_Wi_b, L0_attn_conv_w_b, L0_attn_conv_b_b, L0_attn_dt_bias_b, L0_attn_A_log_b, L0_attn_D_b, L0_attn_norm_w_b, L0_attn_Wo_b, L0_ffn_router_w, L0_ffn_expert_bias, L0_ffn_w_gate, L0_ffn_w_down, L0_ffn_w_gate_shared, L0_ffn_w_down_shared):

    def _L0_attn_ref(u, Wi_f, conv_w_f, conv_b_f, dt_bias_f, A_log_f, D_f, norm_w_f, Wo_f, Wi_b, conv_w_b, conv_b_b, dt_bias_b, A_log_b, D_b, norm_w_b, Wo_b):
        import jax, jax.numpy as jnp
        import numpy as np
        D_MODEL = 128
        D_STATE = 128
        D_CONV = 4
        EXPAND = 2
        D_INNER = EXPAND * D_MODEL
        HEADDIM = 64
        NHEADS = D_INNER // HEADDIM
        NGROUPS = 1
        CONV_DIM = D_INNER + 2 * NGROUPS * D_STATE
        D_IN_PROJ = 2 * D_INNER + 2 * NGROUPS * D_STATE + NHEADS
        BATCH, SEQLEN = (2, 256)

        def _mamba2(u, Wi, conv_w, conv_b, dt_bias, A_log, D, norm_w, Wo):
            b, L, _ = u.shape
            zxbcdt = u @ Wi.T
            z = zxbcdt[..., :D_INNER]
            xBC = zxbcdt[..., D_INNER:D_INNER + CONV_DIM]
            dt = zxbcdt[..., D_INNER + CONV_DIM:]
            xBC_t = jnp.moveaxis(xBC, 1, 2)
            xBC_t = jnp.pad(xBC_t, ((0, 0), (0, 0), (D_CONV - 1, 0)))
            conv = jax.lax.conv_general_dilated(xBC_t, conv_w, (1,), 'VALID', feature_group_count=CONV_DIM, dimension_numbers=('NCH', 'OIH', 'NCH'))
            xBC = jax.nn.silu(jnp.moveaxis(conv, 1, 2) + conv_b)
            x = xBC[..., :D_INNER].reshape(b, L, NHEADS, HEADDIM)
            Bm = xBC[..., D_INNER:D_INNER + NGROUPS * D_STATE].reshape(b, L, D_STATE)
            Cm = xBC[..., D_INNER + NGROUPS * D_STATE:].reshape(b, L, D_STATE)
            dt = jax.nn.softplus(dt + dt_bias)
            A = -jnp.exp(A_log)

            def step(h, inp):
                x_t, B_t, C_t, dt_t = inp
                dA = jnp.exp(dt_t * A)
                h = h * dA[..., None, None] + (dt_t[..., None] * x_t)[..., None] * B_t[:, None, None, :]
                y_t = jnp.einsum('bhpn,bn->bhp', h, C_t)
                return (h, y_t)
            h0 = jnp.zeros((b, NHEADS, HEADDIM, D_STATE), u.dtype)
            xs = (jnp.moveaxis(x, 1, 0), jnp.moveaxis(Bm, 1, 0), jnp.moveaxis(Cm, 1, 0), jnp.moveaxis(dt, 1, 0))
            _, ys = jax.lax.scan(step, h0, xs)
            y = jnp.moveaxis(ys, 0, 1) + D[None, None, :, None] * x
            y = y.reshape(b, L, D_INNER)
            y = y * jax.nn.silu(z)
            y = y * jax.lax.rsqrt(jnp.mean(y * y, axis=-1, keepdims=True) + 1e-05) * norm_w
            return y @ Wo.T
        out_f = _mamba2(u, Wi_f, conv_w_f, conv_b_f, dt_bias_f, A_log_f, D_f, norm_w_f, Wo_f)
        out_b = _mamba2(u[:, ::-1], Wi_b, conv_w_b, conv_b_b, dt_bias_b, A_log_b, D_b, norm_w_b, Wo_b)
        return (out_f + out_b[:, ::-1]) * 0.5

    def _L0_ffn_ref(hidden_states, router_w, expert_bias, w_gate, w_down, w_gate_shared, w_down_shared):
        import jax, jax.numpy as jnp
        import numpy as np
        NUM_EXPERTS = 160
        TOP_K = 8
        ROUTED_SCALE = 2.5
        HIDDEN = 128
        INTER = 64
        B, S, H = hidden_states.shape
        x = hidden_states.reshape(-1, H)
        T = x.shape[0]
        logits = x @ router_w.T + expert_bias[None, :]
        probs = jax.nn.sigmoid(logits)
        top_w, top_idx = jax.lax.top_k(probs, TOP_K)
        top_w = top_w / (jnp.sum(top_w, axis=-1, keepdims=True) + 1e-09)
        top_w = top_w * ROUTED_SCALE
        combine = jnp.zeros((T, NUM_EXPERTS), dtype=x.dtype)
        combine = combine.at[jnp.arange(T)[:, None], top_idx].set(top_w)
        h1 = jax.nn.silu(jnp.einsum('th,eih->eti', x, w_gate))
        h1w = h1 * combine.T[:, :, None]
        routed = jnp.einsum('eti,ehi->th', h1w, w_down)
        shared = jax.nn.silu(x @ w_gate_shared.T) @ w_down_shared.T
        return (routed + shared).reshape(B, S, H)
    x = L0_attn_u
    xn = _layernorm(x, axis=-1)
    s = _L0_attn_ref(xn, L0_attn_Wi_f, L0_attn_conv_w_f, L0_attn_conv_b_f, L0_attn_dt_bias_f, L0_attn_A_log_f, L0_attn_D_f, L0_attn_norm_w_f, L0_attn_Wo_f, L0_attn_Wi_b, L0_attn_conv_w_b, L0_attn_conv_b_b, L0_attn_dt_bias_b, L0_attn_A_log_b, L0_attn_D_b, L0_attn_norm_w_b, L0_attn_Wo_b)
    g = _silu(_L0_ffn_ref(xn, L0_ffn_router_w, L0_ffn_expert_bias, L0_ffn_w_gate, L0_ffn_w_down, L0_ffn_w_gate_shared, L0_ffn_w_down_shared))
    x = x + s * g
    return x

_drawn_inputs = setup_inputs


def setup_inputs(seed=0):
    import zlib

    import numpy as np

    out = dict(_drawn_inputs(seed))
    spreads = {'L0_attn_conv_b_f': (0.0, 0.8),
     'L0_attn_D_f': (1.0, 0.6),
     'L0_attn_norm_w_f': (1.0, 0.6),
     'L0_attn_conv_b_b': (0.0, 0.8),
     'L0_attn_D_b': (1.0, 0.6),
     'L0_attn_norm_w_b': (1.0, 0.6),
     'L0_ffn_expert_bias': (0.0, 0.8)}
    factors = {'L0_attn_Wi_f': 8.0,
     'L0_attn_conv_w_f': 8.0,
     'L0_attn_dt_bias_f': 8.0,
     'L0_attn_A_log_f': 8.0,
     'L0_attn_Wo_f': 8.0,
     'L0_attn_Wi_b': 8.0,
     'L0_attn_conv_w_b': 8.0,
     'L0_attn_dt_bias_b': 8.0,
     'L0_attn_A_log_b': 8.0,
     'L0_attn_Wo_b': 8.0,
     'L0_ffn_router_w': 8.0,
     'L0_ffn_w_gate': 8.0,
     'L0_ffn_w_down': 8.0,
     'L0_ffn_w_gate_shared': 8.0,
     'L0_ffn_w_down_shared': 8.0}
    for name, (base, spread) in spreads.items():
        noise = np.random.default_rng([zlib.crc32(name.encode()), seed]).standard_normal(out[name].shape)
        drawn = base * np.exp(spread * noise) if base else spread * noise
        out[name] = jnp.asarray(drawn.astype(out[name].dtype))
    for name, factor in factors.items():
        out[name] = (out[name] * factor).astype(out[name].dtype)
    return out
```

```python
from contextlib import ExitStack

import numpy as np
import concourse.bass as bass
from concourse import mybir

F32, F16, BF16, I32 = mybir.dt.float32, mybir.dt.float16, mybir.dt.bfloat16, mybir.dt.int32
ALU = mybir.AluOpType
ACT = mybir.ActivationFunctionType
AX = mybir.AxisListType
ds = bass.ds

P = 128
BATCH, SEQ, DM = 8, 1024, 128
TOKENS = BATCH * SEQ
TILES = TOKENS // P
BLK = 512
NBLK = TOKENS // BLK
TPB = BLK // P
SS = 256
NSS = TOKENS // SS
HALO = 4
SW = SS + 2 * HALO
NE, INTER = 160, 64
NQ = 4
EQ = NE // NQ
NIT = EQ // 2
UNITS = NQ * NIT + 1
NH, HD, DS, DI = 4, 64, 128, 256
NCONV = 4
XSCALE = 64.0
WTOP = 1024.0
RMAX = bass.bass_isa.ReduceOp.max


class Memory:
    pass


def need(eng, sem, count):
    if not isinstance(count, int) or count > 0:
        eng.wait_ge(sem, count)


def scale_weights(nc, m):
    with ExitStack() as ctx:
        def sem(name):
            return ctx.enter_context(nc.semaphore(name))

        NCH, CH = 4, NE * INTER // 4
        wstage = ctx.enter_context(nc.sbuf_tensor("wstage", [P, NE * INTER], F32))
        shared = ctx.enter_context(nc.sbuf_tensor("shared", [P, 2, P], F32))
        part_max = ctx.enter_context(nc.sbuf_tensor("part_max", [P, 2, NCH + 2], F32))
        row_max = ctx.enter_context(nc.sbuf_tensor("row_max", [P, 2], F32))
        all_max = ctx.enter_context(nc.sbuf_tensor("all_max", [P, 2], F32))
        pow2 = ctx.enter_context(nc.sbuf_tensor("pow2", [P, 2], F32))
        up = ctx.enter_context(nc.sbuf_tensor("up", [P, 2], F32))
        loaded = [sem(f"wchunk_loaded{c}") for c in range(NCH)]
        shared_loaded = sem("shared_loaded")
        shared_zero = sem("shared_zero")
        maxed = sem("row_max_done")
        reduced = sem("all_max_done")
        scaled = sem("scales_done")
        high_done = sem("high_done")
        low_done = sem("low_done")
        step = sem("vector_step")
        pool_step = sem("pool_step")
        hi = [m.wg_hi, m.wd_hi]
        lo = [m.wg_lo, m.wd_lo]
        src = [m.dram.w_gate, m.dram.w_down]
        block = ctx.enter_context(nc.Block())

        def chunk(c):
            return slice(c * CH, (c + 1) * CH)

        @block.sync
        def _(sp):
            sp.wait_ge(shared_zero, 1)
            sp.dma_start(shared[:, 0, 0:INTER], m.dram.w_gate_shared).then_inc(shared_loaded, 16)
            sp.dma_start(shared[0:INTER, 1, :], m.dram.w_down_shared).then_inc(shared_loaded, 16)
            for w in range(2):
                for c in range(NCH):
                    if w == 1:
                        sp.wait_ge(low_done, c + 1)
                    sp.dma_start(wstage[:, chunk(c)], src[w][:, chunk(c)]).then_inc(loaded[c], 16)

        @block.vector
        def _(dve):
            n = [0]

            def link(ins):
                n[0] += 1
                ins.then_inc(step, 1)
                dve.wait_ge(step, n[0])

            nc.vector.memset(shared[:], 0.0).then_inc(shared_zero, 1)
            link(nc.vector.memset(part_max[:, :, NCH + 1:], 1e-30))
            dve.wait_ge(shared_loaded, 32)
            for w in range(2):
                nc.vector.tensor_reduce(part_max[:, w, NCH:NCH + 1], shared[:, w, :], AX.X, ALU.max,
                                        apply_absolute_value=True)
            for w in range(2):
                for c in range(NCH):
                    dve.wait_ge(loaded[c], 16 * (w + 1))
                    last = nc.vector.tensor_reduce(part_max[:, w, c:c + 1], wstage[:, chunk(c)], AX.X, ALU.max,
                                                   apply_absolute_value=True)
                link(last)
                nc.vector.tensor_reduce(row_max[:, w:w + 1], part_max[:, w, :], AX.X,
                                        ALU.max).then_inc(maxed, 1)
                dve.wait_ge(reduced, w + 1)
                link(nc.vector.tensor_scalar(pow2[:, w:w + 1].bitcast(I32), all_max[:, w:w + 1].bitcast(I32),
                                             0x7F800000, None, ALU.bitwise_and))
                link(nc.vector.reciprocal(up[:, w:w + 1], pow2[:, w:w + 1]))
                link(nc.vector.tensor_scalar(up[:, w:w + 1], up[:, w:w + 1], WTOP, None, ALU.mult))
                if w == 0:
                    nc.vector.tensor_scalar(m.gate_back[:], pow2[:, 0:1], 1.0 / (XSCALE * WTOP), None, ALU.mult)
                    link(nc.vector.reciprocal(m.kappa[:], pow2[:, 0:1]))
                    nc.vector.tensor_scalar(m.kappa[:], m.kappa[:], 64.0, None,
                                            ALU.mult).then_inc(scaled, 1)
                else:
                    nc.vector.tensor_tensor(m.moe_back[:], pow2[:, 0:1], pow2[:, 1:2],
                                            ALU.mult).then_inc(scaled, 1)
                for c in range(NCH):
                    dve.wait_ge(high_done, w * (NCH + 1) + c + 1)
                    nc.vector.scalar_tensor_tensor(lo[w][:, chunk(c)], wstage[:, chunk(c)], up[:, w:w + 1],
                                                   hi[w][:, chunk(c)], ALU.mult,
                                                   ALU.subtract).then_inc(low_done, 1)
                dve.wait_ge(high_done, (w + 1) * (NCH + 1))
                nc.vector.scalar_tensor_tensor(m.sh_lo[:, w, :], shared[:, w, :], up[:, w:w + 1],
                                               m.sh_hi[:, w, :], ALU.mult, ALU.subtract)
            dve.wait_ge(scaled, 2)
            nc.vector.tensor_scalar(m.moe_back[:], m.moe_back[:], 1.0 / (64.0 * WTOP), None, ALU.mult)

        @block.gpsimd
        def _(pool):
            sel = m.pair_select[:].rearrange("p (e j) -> p e j", j=INTER)
            nc.gpsimd.memset(m.pair_select[:], 0.0).then_inc(pool_step, 1)
            pool.wait_ge(pool_step, 1)
            for k, first in enumerate((0, EQ)):
                nc.gpsimd.affine_select(out=sel, in_=sel, compare_op=ALU.not_equal, fill=1.0, base=-first,
                                        pattern=[[-1, EQ], [0, INTER]],
                                        channel_multiplier=1).then_inc(pool_step, 1)
                pool.wait_ge(pool_step, k + 2)
            nc.gpsimd.memset(m.ident[:], 0.0).then_inc(pool_step, 1)
            pool.wait_ge(pool_step, 4)
            nc.gpsimd.affine_select(out=m.ident[:], in_=m.ident[:], compare_op=ALU.not_equal, fill=1.0, base=0,
                                    pattern=[[-1, P]], channel_multiplier=1).then_inc(pool_step, 1)
            pool.wait_ge(pool_step, 5)
            nc.gpsimd.tensor_copy(m.ident16[:], m.ident[:])
            nc.gpsimd.memset(m.minus_half[:], -0.5)
            nc.gpsimd.memset(m.eps[:], 1e-5)
            for t in (m.xhi, m.xlo):
                for b in range(BATCH):
                    nc.gpsimd.memset(t[:, 4 * b, 0:HALO], 0.0)
                    nc.gpsimd.memset(t[:, 4 * b + 3, SW - HALO:SW], 0.0)
            for w in range(2):
                pool.wait_ge(maxed, w + 1)
                nc.gpsimd.partition_all_reduce(all_max[:, w:w + 1], row_max[:, w:w + 1], P,
                                               RMAX).then_inc(reduced, 1)

        @block.scalar
        def _(act):
            for w in range(2):
                act.wait_ge(scaled, w + 1)
                for c in range(NCH):
                    nc.scalar.activation(hi[w][:, chunk(c)], wstage[:, chunk(c)], ACT.Copy,
                                         scale=up[:, w:w + 1]).then_inc(high_done, 1)
                nc.scalar.activation(m.sh_hi[:, w, :], shared[:, w, :], ACT.Copy,
                                     scale=up[:, w:w + 1]).then_inc(high_done, 1)


def prepare_tokens(nc, m):
    with ExitStack() as ctx:
        def sem(name):
            return ctx.enter_context(nc.semaphore(name))

        def sb(name, shape, dt=F32):
            return ctx.enter_context(nc.sbuf_tensor("tok_" + name, shape, dt))

        def ps(name, shape, dt=F32):
            return ctx.enter_context(nc.psum_tensor("tok_" + name, shape, dt))

        x_sb = sb("x_sb", [P, 2, TPB, DM])
        warm = sb("warm", [P, 1])
        stats = sb("stats", [P, TPB, 6])
        mv = sb("mv", [P, TPB, 2])
        var_eps = sb("var_eps", [P, TPB])
        rstd = sb("rstd", [P, TPB])
        xn = sb("xn", [P, TPB, DM])
        xt = sb("xt", [P, BLK])
        router = sb("router", [P, NE])
        w_dt = sb("w_dt", [P, 36])
        bias = sb("bias", [P, 2, NE])
        logits = sb("logits", [P, TPB, NE])
        probs = sb("probs", [P, TPB, NE])
        top8 = sb("top8", [P, TPB, 8])
        rest = sb("rest", [P, TPB, NE])
        picked = sb("picked", [P, TPB, NE])
        wsum = sb("wsum", [P, TPB])
        wnorm = sb("wnorm", [P, TPB])
        comb = sb("comb", [P, TPB, NE])
        parts = sb("parts", [P, TPB, NQ, 2, EQ], F16)
        comb_t = sb("comb_t", [2 * EQ, NQ, BLK], F16)
        dt_raw = sb("dt_raw", [36, BLK])
        xt_ps = ps("xt_ps", [P, BLK])
        logit_ps = [ps(f"logit_ps{i}", [P, 2, NE]) for i in range(2)]
        dt_ps = ps("dt_ps", [36, BLK])
        comb_ps = [ps(f"comb_ps{i}", [2 * EQ, 2, BLK], F16) for i in range(2)]

        params = sem("params_loaded")
        w_dt_zero = sem("w_dt_zero")
        step = sem("vector_step")
        apart = sem("apart")
        x_loaded = [sem(f"x_loaded{h}") for h in range(2)]
        x_free = sem("x_free")
        var_done = sem("var_done")
        rstd_done = sem("rstd_done")
        xn_done = sem("xn_done")
        xt_ready = sem("xt_ready")
        xt_copied = sem("xt_copied")
        xhi_done = sem("xhi_done")
        xlo_done = sem("xlo_done")
        halo_done = sem("halo_done")
        logits_ready = sem("logits_ready")
        logits_done = sem("logits_done")
        dt_ready = sem("dt_ready")
        dt_copied = sem("dt_copied")
        dt_stored = sem("dt_stored")
        probs_done = sem("probs_done")
        comb_done = sem("comb_done")
        comb_hi_done = sem("comb_hi_done")
        parts_done = sem("parts_done")
        comb_t_ready = sem("comb_t_ready")
        comb_t_done = sem("comb_t_done")
        comb_stored = sem("comb_stored")
        PAIRS = NBLK // 2
        NPARAM = 16 * 5
        block = ctx.enter_context(nc.Block())

        def loop(eng, body, count):
            body(0)
            with eng.Fori(1, count) as i:
                body(i)

        @block.sync
        def _(sp):
            sp.wait_ge(w_dt_zero, 1)
            sp.dma_start(router[:], m.dram.router).then_inc(params, 16)
            for d in range(2):
                sp.dma_start(w_dt[:, 32 * d:32 * d + NH], m.dram.w_in[d][:, 3 * DI:]).then_inc(params, 16)
            for k in range(2):
                sp.dma_start(bias[:, k, :], m.dram.expert_bias).then_inc(params, 16)
            def pair(i):
                for h in range(2):
                    b = 2 * i + h
                    need(sp, x_free, b - 1)
                    sp.dma_start(x_sb[:, h], m.dram.x_blocks[ds(b, 1)].rearrange("o p j d -> p (o j) d")
                                 ).then_inc(x_loaded[h], 16)

            loop(sp, pair, PAIRS)

        @block.gpsimd
        def _(pool):
            def pair(i):
                for h in range(2):
                    b = 2 * i + h
                    pool.wait_ge(var_done, b + 1)
                    nc.gpsimd.tensor_tensor(rstd[:], var_eps[:], m.minus_half[:, 0:TPB],
                                            ALU.pow).then_inc(rstd_done, 1)
                    pool.wait_ge(xhi_done, b + 1)
                    pool.wait_ge(xlo_done, b + 1)
                    for t in (m.xhi, m.xlo):
                        left, right = t[:, ds(2 * b, 1)], t[:, ds(2 * b + 1, 1)]
                        nc.gpsimd.tensor_copy(left[:, :, HALO + SS:], right[:, :, HALO:2 * HALO])
                        nc.gpsimd.tensor_copy(right[:, :, 0:HALO], left[:, :, SS:SS + HALO])
                        if h == 0:
                            nxt = t[:, ds(2 * b + 2, 1)]
                            nc.gpsimd.tensor_copy(nxt[:, :, 0:HALO], right[:, :, SS:SS + HALO])
                        else:
                            prev = t[:, ds(2 * b - 1, 1)]
                            nc.gpsimd.tensor_copy(prev[:, :, HALO + SS:], left[:, :, HALO:2 * HALO])
                    pool.wait_ge(dt_copied, b + 1)
                    pool.dma_start(m.dram.dt_scratch[ds(b, 1)].rearrange("o r t -> (o r) t"),
                                   dt_raw[:]).then_inc(dt_stored, 16)
                    pool.wait_ge(comb_t_done, 2 * b + 2)
                    pool.dma_start(m.dram.comb_scratch[ds(b, 1)].rearrange("o r q t -> (o r) q t"),
                                   comb_t[:]).then_inc(comb_stored, 16)

            loop(pool, pair, PAIRS)
            pool.wait_ge(dt_stored, 16 * NBLK)
            pool.wait_ge(comb_stored, 16 * NBLK)

        @block.vector
        def _(dve):
            nc.vector.memset(w_dt[:], 0.0).then_inc(w_dt_zero, 1)
            dve.wait_ge(params, NPARAM)
            LINKS = 8

            def block_steps(b, h, i):
                n = [0]

                def link(ins):
                    n[0] += 1
                    ins.then_inc(step, 1)
                    dve.wait_ge(step, LINKS * b + n[0])

                dve.wait_ge(x_loaded[h], 16 * (i + 1))
                for j in range(TPB):
                    last = nc.vector.bn_stats(stats[:, j, :], x_sb[:, h, j, :])
                link(last)
                dve.sem_inc(apart, 1)
                for j in range(TPB):
                    last = nc.vector.bn_aggr(mv[:, j, :], stats[:, j, :])
                link(last)
                nc.vector.tensor_scalar(var_eps[:], mv[:, :, 1], 1e-5, None, ALU.add).then_inc(var_done, 1)
                dve.wait_ge(rstd_done, b + 1)
                need(dve, xt_ready, b)
                for j in range(TPB):
                    last = nc.vector.tensor_scalar(xn[:, j, :], x_sb[:, h, j, :], mv[:, j, 0:1], rstd[:, j:j + 1],
                                                   ALU.subtract, ALU.mult)
                    last.then_inc(xn_done, 1)
                dve.wait_ge(xn_done, TPB * (b + 1))
                dve.sem_inc(x_free, 1)
                dve.wait_ge(xhi_done, b + 1)
                nc.vector.scalar_tensor_tensor(m.xlo[:, ds(2 * b, 2), HALO:HALO + SS],
                                               xt_ps[:].rearrange("p (s t) -> p s t", t=SS), XSCALE,
                                               m.xhi[:, ds(2 * b, 2), HALO:HALO + SS],
                                               ALU.mult, ALU.subtract).then_inc(xlo_done, 1)
                dve.wait_ge(logits_ready, b + 1)
                for k in range(2):
                    last = nc.vector.tensor_tensor(logits[:, 2 * k:2 * k + 2, :], logit_ps[k][:], bias[:], ALU.add)
                last.then_inc(logits_done, 1)
                dve.wait_ge(probs_done, b + 1)
                dve.sem_inc(apart, 1)
                for j in range(TPB):
                    last = nc.vector.max(top8[:, j, :], probs[:, j, :])
                link(last)
                dve.sem_inc(apart, 1)
                for j in range(TPB):
                    nc.vector.match_replace(rest[:, j, :], top8[:, j, :], probs[:, j, :], 0.0)
                link(nc.vector.tensor_reduce(wsum[:], top8[:], AX.X, ALU.add))
                link(nc.vector.tensor_scalar(wsum[:], wsum[:], 1e-9, None, ALU.add))
                link(nc.vector.reciprocal(wnorm[:], wsum[:]))
                nc.vector.tensor_tensor(picked[:], probs[:], rest[:], ALU.subtract)
                link(nc.vector.tensor_scalar(wnorm[:], wnorm[:], m.kappa[:, 0:1], 2.5, ALU.mult, ALU.mult))
                for j in range(TPB):
                    last = nc.vector.tensor_scalar(comb[:, j, :], picked[:, j, :], wnorm[:, j:j + 1], None, ALU.mult)
                link(last)
                assert n[0] == LINKS
                dve.sem_inc(comb_done, 1)
                dve.wait_ge(comb_hi_done, b + 1)
                nc.vector.tensor_tensor(parts[:, :, :, 1, :], comb[:].rearrange("p j (q e) -> p j q e", q=NQ),
                                        parts[:, :, :, 0, :], ALU.subtract).then_inc(parts_done, 1)

            def pair(i):
                for h in range(2):
                    block_steps(2 * i + h, h, i)

            loop(dve, pair, PAIRS)

        @block.scalar
        def _(act):
            def block_steps(b):
                act.wait_ge(xt_ready, b + 1)
                need(act, dt_ready, b)
                nc.scalar.activation(xt[:], xt_ps[:], ACT.Copy).then_inc(xt_copied, 1)
                nc.scalar.activation(m.xhi[:, ds(2 * b, 2), HALO:HALO + SS],
                                     xt_ps[:].rearrange("p (s t) -> p s t", t=SS), ACT.Copy,
                                     scale=XSCALE).then_inc(xhi_done, 1)
                act.wait_ge(dt_ready, b + 1)
                need(act, dt_stored, 16 * b)
                nc.scalar.activation(dt_raw[:], dt_ps[:], ACT.Copy).then_inc(dt_copied, 1)
                act.wait_ge(logits_done, b + 1)
                need(act, comb_done, b)
                nc.scalar.activation(probs[:], logits[:], ACT.Sigmoid).then_inc(probs_done, 1)
                act.wait_ge(comb_done, b + 1)
                need(act, comb_t_ready, 2 * b)
                nc.scalar.activation(parts[:, :, :, 0, :], comb[:].rearrange("p j (q e) -> p j q e", q=NQ),
                                     ACT.Copy).then_inc(comb_hi_done, 1)
                need(act, comb_stored, 16 * b)
                for k in range(2):
                    act.wait_ge(comb_t_ready, 2 * b + k + 1)
                    nc.scalar.activation(comb_t[:, 2 * k:2 * k + 2, :], comb_ps[k][:],
                                         ACT.Copy).then_inc(comb_t_done, 1)

            nc.scalar.activation(warm[:], m.minus_half[:, 0:1], ACT.Sigmoid)
            loop(act, block_steps, NBLK)

        @block.tensor
        def _(pe):
            pe.wait_ge(params, NPARAM)
            def block_steps(b):
                pe.wait_ge(xn_done, TPB * (b + 1))
                need(pe, xlo_done, b)
                for j in range(TPB):
                    last = nc.tensor.transpose(xt_ps[:, j * P:(j + 1) * P], xn[:, j, :], m.ident[:])
                last.then_inc(xt_ready, 1)
                pe.wait_ge(xt_copied, b + 1)
                need(pe, logits_done, b)
                for j in range(TPB):
                    last = nc.tensor.matmul(logit_ps[j // 2][:, j % 2, :], xt[:, j * P:(j + 1) * P], router[:],
                                            start=True, stop=True)
                last.then_inc(logits_ready, 1)
                need(pe, dt_copied, b)
                nc.tensor.matmul(dt_ps[:], w_dt[:], xt[:], start=True, stop=True).then_inc(dt_ready, 1)
                pe.wait_ge(parts_done, b + 1)
                for k in range(2):
                    need(pe, comb_t_done, 2 * b + k)
                    for q in (2 * k, 2 * k + 1):
                        for j in range(TPB):
                            last = nc.tensor.transpose(
                                comb_ps[k][:, q % 2, j * P:(j + 1) * P],
                                parts[:, j, q].rearrange("p a e -> p (a e)"), m.ident16[:])
                    last.then_inc(comb_t_ready, 1)

            loop(pe, block_steps, NBLK)


def run_experts(nc, m):
    with ExitStack() as ctx:
        def sem(name):
            return ctx.enter_context(nc.semaphore(name))

        def sb(name, shape, dt=F32):
            return ctx.enter_context(nc.sbuf_tensor("moe_" + name, shape, dt))

        def ps(name, shape, dt=F32):
            return ctx.enter_context(nc.psum_tensor("moe_" + name, shape, dt))

        comb_t = sb("moe_comb", [2 * EQ, 2, NQ, BLK], F16)
        act_out = [sb(f"silu{k}", [P, BLK]) for k in range(2)]
        prod = [sb(f"prod{k}", [P, BLK]) for k in range(2)]
        h_hi = [sb(f"h_hi{q}", [P, BLK], F16) for q in range(NQ)]
        h_lo = [sb(f"h_lo{q}", [P, BLK], F16) for q in range(NQ)]
        hs_hi = sb("hs_hi", [INTER, BLK], F16)
        hs_lo = sb("hs_lo", [INTER, BLK], F16)
        gate_t = sb("gate_t", [P, BLK])
        up_ps = [ps(f"up_ps{k}", [P, BLK]) for k in range(2)]
        spread_ps = [ps(f"spread_ps{k}", [P, BLK]) for k in range(2)]
        sum_ps = [ps(f"sum_ps{k}", [P, BLK]) for k in range(2)]
        back_ps = ps("back_ps", [P, TPB, DM])

        comb_loaded = [sem(f"comb_loaded{k}") for k in range(2)]
        up_done = sem("up_done")
        spread_done = sem("spread_done")
        silu_done = sem("silu_done")
        prod_done = sem("prod_done")
        hi_done = sem("hi_done")
        lo_done = sem("lo_done")
        down_done = sem("down_done")
        gate_t_done = sem("gate_t_done")
        back_ready = sem("back_ready")
        back_copied = sem("back_copied")
        block = ctx.enter_context(nc.Block())

        SH = "shared"

        def blocks(eng, body):
            body(0, 0, True)
            with eng.Fori(0, (NBLK - 2) // 2) as i:
                for h in range(2):
                    body(2 * i + 1 + h, (1 + h) % 2, False)
            body(NBLK - 1, (NBLK - 1) % 2, False)

        def parity(bp, q):
            return (bp + 1 + q) % 2

        @block.sync
        def _(sp):
            def load(b, bp):
                sp.dma_start(comb_t[:, bp], m.dram.comb_scratch[ds(b, 1)].rearrange("o r q t -> (o r) q t")
                             ).then_inc(comb_loaded[bp], 16)

            load(0, 0)
            load(1, 1)
            with sp.Fori(1, NBLK // 2) as i:
                for bp in range(2):
                    sp.wait_ge(spread_done, (2 * i + bp - 1) * (UNITS - 1))
                    load(2 * i + bp, bp)

        @block.tensor
        def _(pe):
            def rhs(t, b):
                return t[:, ds(2 * b, 2), HALO:HALO + SS]

            def up(b, bp, K, k, wh, wl, rows=P):
                if K is not None:
                    pe.wait_ge(silu_done, K - 1)
                out = up_ps[k][0:rows].rearrange("p (s t) -> p s t", t=SS)
                nc.tensor.matmul(out, wh, rhs(m.xhi, b), start=True, stop=False)
                nc.tensor.matmul(out, wh, rhs(m.xlo, b), start=False, stop=False)
                nc.tensor.matmul(out, wl, rhs(m.xhi, b), start=False, stop=True).then_inc(up_done, 1)

            def up_unit(b, bp, it, q):
                K = UNITS * b + 1 + NQ * it + q
                at = (NIT * q + it) * P
                early = isinstance(b, int) and isinstance(it, int) and K < 2
                up(b, bp, None if early else K, parity(bp, q), m.wg_hi[:, ds(at, P)], m.wg_lo[:, ds(at, P)])
                if not early:
                    pe.wait_ge(prod_done, K - 1)
                nc.tensor.matmul(spread_ps[q % 2][:], m.pair_select[:, ds(it * P, P)], comb_t[:, bp, q, :],
                                 start=True, stop=True).then_inc(spread_done, 1)

            def down(bp, K, wh, wl, hh, hl, start, stop):
                pe.wait_ge(lo_done, K + 1)
                nc.tensor.matmul(sum_ps[bp][:], wh, hh, start=start, stop=False)
                nc.tensor.matmul(sum_ps[bp][:], wh, hl, start=False, stop=False)
                nc.tensor.matmul(sum_ps[bp][:], wl, hh, start=False,
                                 stop=stop).then_inc(down_done, 1)

            def down_unit(b, bp, it, q, stop=False):
                at = (NIT * q + it) * P
                down(bp, UNITS * b + 1 + NQ * it + q, m.wd_hi[:, ds(at, P)], m.wd_lo[:, ds(at, P)],
                     h_hi[q][:], h_lo[q][:], False, stop)

            def to_tokens(n):
                pe.wait_ge(gate_t_done, n + 2)
                pe.wait_ge(back_copied, n + 1)
                for j in range(TPB):
                    last = nc.tensor.transpose(back_ps[:, j, :], gate_t[:, j * P:(j + 1) * P], m.ident[:])
                last.then_inc(back_ready, 1)

            def body(b, bp, first):
                pe.wait_ge(comb_loaded[bp], 16 * (b // 2 + 1) if isinstance(b, int) else comb_target(b, bp))
                K = UNITS * b
                up(b, bp, None if first else K, bp, m.sh_hi[:, 0, 0:INTER], m.sh_lo[:, 0, 0:INTER], rows=INTER)
                for q in range(NQ):
                    up_unit(b, bp, 0, q)
                    if not first:
                        down_unit(b - 1, 1 - bp, NIT - 1, q, stop=q == NQ - 1)
                if not first:
                    pe.wait_ge(gate_t_done, b)
                down(bp, K, m.sh_hi[0:INTER, 1, :], m.sh_lo[0:INTER, 1, :], hs_hi[:], hs_lo[:], True, False)
                with pe.Fori(1, NIT) as it:
                    for q in range(NQ):
                        up_unit(b, bp, it, q)
                        down_unit(b, bp, it - 1, q)
                if not first:
                    to_tokens(b - 1)

            def comb_target(b, bp):
                return 8 * (b - bp) + 16

            pe.sem_inc(back_ready, 1)
            blocks(pe, body)
            b, bp = NBLK - 1, (NBLK - 1) % 2
            for q in range(NQ):
                down_unit(b, bp, NIT - 1, q, stop=q == NQ - 1)
            to_tokens(b)

        @block.scalar
        def _(act):
            def silu(K, k, rows=P, early=False):
                act.wait_ge(up_done, K + 1)
                if not early:
                    act.wait_ge(prod_done, K - 1)
                nc.scalar.activation(act_out[k][0:rows], up_ps[k][0:rows], ACT.Silu,
                                     scale=m.gate_back[0:rows, 0:1]).then_inc(silu_done, 1)

            def high(K, k, out, rows, free):
                act.wait_ge(prod_done, K + 1)
                if free is not None:
                    act.wait_ge(down_done, free)
                nc.scalar.activation(out[0:rows], prod[k][0:rows], ACT.Copy).then_inc(hi_done, 1)

            def gate(b, bp):
                act.wait_ge(down_done, UNITS * (b + 1))
                act.wait_ge(back_ready, b + 1)
                nc.scalar.activation(gate_t[:], sum_ps[bp][:], ACT.Silu,
                                     scale=m.moe_back[:, 0:1]).then_inc(gate_t_done, 1)

            def body(b, bp, first):
                K = UNITS * b
                silu(K, bp, INTER, early=first)
                if not first:
                    high(K - 1, parity(1 - bp, NQ - 1), h_hi[NQ - 1], P, K - 1 - NQ + 1)
                for q in range(NQ):
                    silu(K + 1 + q, parity(bp, q), early=first and q == 0)
                    if q == 0:
                        high(K, bp, hs_hi, INTER, None if first else K - UNITS + 1)
                    else:
                        high(K + q, parity(bp, q - 1), h_hi[q - 1], P, None if first else K - NQ + q)
                if not first:
                    gate(b - 1, 1 - bp)
                with act.Fori(1, NIT) as it:
                    for q in range(NQ):
                        k = K + 1 + NQ * it + q
                        silu(k, parity(bp, q))
                        if q == 0:
                            prev_free(b, bp, it, k)
                        else:
                            high(k - 1, parity(bp, q - 1), h_hi[q - 1], P, k - 1 - NQ + 1)

            def prev_free(b, bp, it, k):
                high(k - 1, parity(bp, NQ - 1), h_hi[NQ - 1], P, k - 1 - NQ + 1)

            act.sem_inc(gate_t_done, 1)
            blocks(act, body)
            b, bp = NBLK - 1, (NBLK - 1) % 2
            K = UNITS * (b + 1)
            high(K - 1, parity(bp, NQ - 1), h_hi[NQ - 1], P, K - 1 - NQ + 1)
            gate(b, bp)

        @block.gpsimd
        def _(pool):
            def low(K, k, out, high, rows=P):
                pool.wait_ge(hi_done, K + 1)
                nc.gpsimd.tensor_tensor(out[0:rows], prod[k][0:rows], high[0:rows],
                                        ALU.subtract).then_inc(lo_done, 1)

            def body(b, bp, first):
                K = UNITS * b
                low(K, bp, hs_lo, hs_hi, INTER)
                with pool.Fori(0, NIT) as it:
                    for q in range(NQ):
                        low(K + 1 + NQ * it + q, parity(bp, q), h_lo[q], h_hi[q])

            blocks(pool, body)

        @block.vector
        def _(dve):
            def weigh(b, bp, it, q, early):
                K = UNITS * b + 1 + NQ * it + q
                dve.wait_ge(silu_done, K + 1)
                dve.wait_ge(spread_done, (UNITS - 1) * b + NQ * it + q + 1)
                if not early:
                    dve.wait_ge(lo_done, K - 1)
                k = parity(bp, q)
                nc.vector.tensor_tensor(prod[k][:], act_out[k][:], spread_ps[q % 2][:],
                                        ALU.mult).then_inc(prod_done, 1)

            def copy_back(n):
                dve.wait_ge(back_ready, n + 2)
                nc.vector.tensor_copy(m.gate[:, ds(TPB * n, TPB), :], back_ps[:]).then_inc(back_copied, 1)

            def body(b, bp, first):
                K = UNITS * b
                dve.wait_ge(silu_done, K + 1)
                if not first:
                    dve.wait_ge(lo_done, K - 1)
                nc.vector.tensor_scalar(prod[bp][0:INTER], act_out[bp][0:INTER], m.kappa[0:INTER, 0:1], None,
                                        ALU.mult).then_inc(prod_done, 1)
                weigh(b, bp, 0, 0, first)
                for q in range(1, NQ):
                    weigh(b, bp, 0, q, False)
                with dve.Fori(1, NIT) as it:
                    for q in range(NQ):
                        weigh(b, bp, it, q, False)
                if not first:
                    copy_back(b - 1)

            dve.sem_inc(back_copied, 1)
            blocks(dve, body)
            copy_back(NBLK - 1)


def prepare_decays(nc, m):
    with ExitStack() as ctx:
        def sem(name):
            return ctx.enter_context(nc.semaphore(name))

        def sb(name, shape, dt=F32):
            return ctx.enter_context(nc.sbuf_tensor("dec_" + name, shape, dt))

        R, HB, CPB = 2 * NH * BATCH, NH * BATCH, SEQ // P
        bias_r, a_log, a_neg = (sb(n, [R, 1]) for n in ("dt_bias_rows", "a_log_rows", "a_neg"))
        rows = [m.experts[0:R, SEQ * k:SEQ * (k + 1)] for k in range(12)]
        raw, u, e, q, l2, dt, decay, inner, first, prefix = rows[0:10]
        part = [t[:, 0:SEQ] for t in (rows[10].bitcast(BF16), rows[11].bitcast(BF16))]
        part.append(rows[10].bitcast(BF16)[:, SEQ:])
        tot = sb("tot", [R, CPB])
        spread = sb("tot_spread", [R, R, CPB])
        ones = sb("ones", [R, P])
        w_stage = sb("w_stage", [P, 2, 3 * DI])
        w_max, w_all, w_pow2, w_up = (sb(n, [P, 2]) for n in ("w_max", "w_all", "w_pow2", "w_up"))
        back = sb("w_back", [P, 2])
        cw, skip, norm = sb("cw", [P, 2, 4, NCONV]), sb("skip", [P, 2, 2]), sb("norm", [P, 2, 2])
        wo_stage = sb("wo_stage", [P, 2, 2, DM])
        warm = sb("warm", [P, 1])
        tot_ps = ctx.enter_context(nc.psum_tensor("tot_ps", [P, R, CPB], F32))
        dt_ps = ctx.enter_context(nc.psum_tensor("dt_tok_ps", [P, CPB, R], F32))
        pre_ps = ctx.enter_context(nc.psum_tensor("pre_tok_ps", [P, CPB, R], F32))

        loaded, w_loaded, small = sem("rows_loaded"), sem("w_loaded"), sem("small_loaded")
        step, v_done, e_done, dt_done, decay_done = (sem(n) for n in (
            "vector_step", "softplus_in", "exp_done", "dt_done", "decay_done"))
        a_done, prefix_done, spread_done = sem("a_done"), sem("prefix_done"), sem("spread_done")
        parts_done, parts_stored, parts_loaded, tables_ready = (sem(n) for n in (
            "parts_done", "parts_stored", "parts_loaded", "tables_ready"))
        maxed, reduced, up_done, high_done = sem("w_maxed"), sem("w_reduced"), sem("w_up_done"), sem("w_high_done")
        pool_step = sem("pool_step")
        block = ctx.enter_context(nc.Block())

        @block.sync
        def _(sp):
            dt_rows = m.dram.dt_scratch.rearrange("(b k) r t -> r b k t", k=2)
            for d in range(2):
                for h in range(NH):
                    r = HB * d + BATCH * h
                    sp.dma_start(raw[r:r + BATCH, :].rearrange("b (k t) -> b k t", k=2),
                                 dt_rows[32 * d + h]).then_inc(loaded, 16)
            sp.dma_start(bias_r[:], m.dram.dt_bias).then_inc(loaded, 16)
            sp.dma_start(a_log[:], m.dram.a_log).then_inc(loaded, 16)
            for d in range(2):
                sp.dma_start(w_stage[:, d, :], m.dram.w_in[d][:, 0:3 * DI]).then_inc(w_loaded, 16)
            for t, src in ((cw, m.dram.conv_w), (m.conv_b, m.dram.conv_b), (skip, m.dram.skip),
                           (norm, m.dram.norm_w), (wo_stage, m.dram.w_out)):
                sp.dma_start(t[:], src).then_inc(small, 16)
            sp.wait_ge(parts_done, 3)
            for k in range(3):
                sp.dma_start(m.dram.decay_scratch[k], part[k]).then_inc(parts_stored, 16)
            sp.wait_ge(parts_stored, 16 * 3)
            for k in range(3):
                for d in range(2):
                    r = 3 * NH * d + NH * k
                    sp.dma_start(m.decay_parts[r:r + NH, :],
                                 m.dram.decay_scratch[k, HB * d:HB * (d + 1), :]
                                 .rearrange("(h b) t -> h (b t)", h=NH)).then_inc(parts_loaded, 16)
            sp.wait_ge(parts_loaded, 16 * 6)

        @block.vector
        def _(dve):
            n = [0]

            def link(ins):
                n[0] += 1
                ins.then_inc(step, 1)
                dve.wait_ge(step, n[0])

            V = nc.vector
            V.memset(ones[:], 1.0)
            V.memset(m.state[:], 0.0)
            dve.wait_ge(loaded, 16 * 10)
            link(V.tensor_scalar(raw[:], raw[:], bias_r[:, 0:1], None, ALU.add))
            link(V.tensor_scalar(u[:], raw[:], -1.0, None, ALU.mult))
            V.tensor_tensor(u[:], u[:], raw[:], ALU.min).then_inc(v_done, 1)
            dve.wait_ge(e_done, 1)
            link(V.tensor_scalar(u[:], e[:], 2.0, None, ALU.add))
            link(V.reciprocal(u[:], u[:]))
            link(V.tensor_tensor(u[:], e[:], u[:], ALU.mult))
            link(V.tensor_tensor(l2[:], u[:], u[:], ALU.mult))
            link(V.tensor_scalar(q[:], l2[:], 1.0 / 19, None, ALU.mult))
            for k in range(8, 0, -1):
                link(V.scalar_tensor_tensor(q[:], q[:], 1.0 / (2 * k + 1), l2[:], ALU.add, ALU.mult))
            link(V.scalar_tensor_tensor(q[:], q[:], 1.0, u[:], ALU.add, ALU.mult))
            link(V.tensor_scalar(raw[:], raw[:], 0.0, None, ALU.max))
            V.scalar_tensor_tensor(dt[:], q[:], 2.0, raw[:], ALU.mult, ALU.add).then_inc(dt_done, 1)
            dve.wait_ge(a_done, 1)
            V.tensor_scalar(a_neg[:], a_neg[:], -1.0, None, ALU.mult).then_inc(a_done, 1)
            dve.wait_ge(decay_done, 1)
            link(V.tensor_copy(inner[:], decay[:]))
            V.memset(inner[0:HB, 0::P], 0.0)
            link(V.memset(inner[HB:R, P - 1::P], 0.0))
            link(V.tensor_tensor(first[:], decay[:], inner[:], ALU.subtract))
            V.tensor_tensor_scan(prefix[0:HB, :], inner[0:HB, :], first[0:HB, :], 0.0, ALU.mult, ALU.add)
            link(V.tensor_tensor_scan(prefix[HB:R, ::-1], inner[HB:R, ::-1], first[HB:R, ::-1], 0.0,
                                      ALU.mult, ALU.add))
            V.tensor_copy(tot[0:HB, :], prefix[0:HB, P - 1::P])
            link(V.tensor_copy(tot[HB:R, :], prefix[HB:R, 0::P]))
            V.memset(tot[0:HB, 0:1], 0.0)
            V.memset(tot[HB:R, CPB - 1:CPB], 0.0)
            V.memset(prefix[0:HB, 0:P], 0.0)
            link(V.memset(prefix[HB:R, SEQ - P:SEQ], 0.0))
            V.tensor_copy(tot[0:1, 0:1], tot[0:1, 0:1]).then_inc(prefix_done, 1)
            dve.wait_ge(prefix_done, 1)
            V.tensor_tensor(spread[:], m.ident[0:R, 0:R].unsqueeze(2).broadcast_to([R, R, CPB]),
                            tot[:].unsqueeze(1).broadcast_to([R, R, CPB]), ALU.mult).then_inc(spread_done, 1)
            link(V.tensor_copy(part[0][:], inner[:]))
            for k in (1, 2):
                link(V.tensor_tensor(inner[:], inner[:], part[k - 1][:], ALU.subtract))
                link(V.tensor_copy(part[k][:], inner[:]))
            dve.sem_inc(parts_done, 3)
            dve.wait_ge(w_loaded, 32)
            for d in range(2):
                last = V.tensor_reduce(w_max[:, d:d + 1], w_stage[:, d, :], AX.X, ALU.max,
                                       apply_absolute_value=True)
            link(last)
            V.tensor_scalar(w_max[:], w_max[:], 1e-30, None, ALU.max).then_inc(maxed, 1)
            dve.wait_ge(reduced, 1)
            link(V.tensor_scalar(w_pow2[:].bitcast(I32), w_all[:].bitcast(I32), 0x7F800000, None,
                                 ALU.bitwise_and))
            link(V.reciprocal(w_up[:], w_pow2[:]))
            V.tensor_scalar(w_up[:], w_up[:], WTOP, None, ALU.mult).then_inc(up_done, 1)
            link(V.tensor_scalar(m.in_back[:], w_pow2[:], 1.0 / (XSCALE * WTOP), None, ALU.mult))
            dve.wait_ge(small, 16 * 5)
            for d in range(2):
                V.tensor_scalar(m.conv_w[:, d], cw[:, d], m.in_back[:, d:d + 1], None, ALU.mult)
                for k in range(2):
                    V.tensor_scalar(m.skip_diag[:, d, k, :], m.ident[:], skip[:, d, k:k + 1], None, ALU.mult)
                    V.tensor_scalar(m.w_out[:, d, k, :], wo_stage[:, d, k, :], norm[:, d, k:k + 1], 0.5,
                                    ALU.mult, ALU.mult)
            for h in range(NH):
                V.tensor_copy(m.ident4[:, h, :], m.ident[:])
            for d in range(2):
                dve.wait_ge(high_done, d + 1)
                V.scalar_tensor_tensor(m.win_lo[:, d, :], w_stage[:, d, :], w_up[:, d:d + 1],
                                       m.win_hi[:, d, :], ALU.mult, ALU.subtract)
            dve.wait_ge(tables_ready, 3)
            for d in range(2):
                rows = slice(HB * d, HB * (d + 1))
                V.tensor_copy(m.tot[:, d].rearrange("p (b c) h -> p h b c", b=BATCH),
                              tot_ps[:, rows, :].rearrange("p (h b) c -> p h b c", h=NH))
                for t, src in ((m.dt_tok, dt_ps), (m.prefix_tok, pre_ps)):
                    V.tensor_copy(t[:, d].rearrange("p (b c) h -> p h b c", b=BATCH),
                                  src[:, :, rows].rearrange("p c (h b) -> p h b c", h=NH))

        @block.gpsimd
        def _(pool):
            nc.gpsimd.memset(m.head_select[:], 0.0).then_inc(pool_step, 1)
            pool.wait_ge(pool_step, 1)
            for k in range(3):
                nc.gpsimd.affine_select(out=m.head_select[:], in_=m.head_select[:], compare_op=ALU.not_equal,
                                        fill=1.0, base=-NH * k, pattern=[[-3 * NH, 2], [-1, NH], [0, P]],
                                        channel_multiplier=1).then_inc(pool_step, 1)
                pool.wait_ge(pool_step, k + 2)
            pool.wait_ge(maxed, 1)
            nc.gpsimd.partition_all_reduce(w_all[:], w_max[:], P, RMAX).then_inc(reduced, 1)

        @block.scalar
        def _(act):
            nc.scalar.activation(warm[:], m.minus_half[:, 0:1], ACT.Exp)
            act.wait_ge(loaded, 16 * 10)
            nc.scalar.activation(a_neg[:], a_log[:], ACT.Exp).then_inc(a_done, 1)
            act.wait_ge(v_done, 1)
            nc.scalar.activation(e[:], u[:], ACT.Exp).then_inc(e_done, 1)
            act.wait_ge(dt_done, 1)
            act.wait_ge(a_done, 2)
            nc.scalar.activation(decay[:], dt[:], ACT.Exp, scale=a_neg[:, 0:1]).then_inc(decay_done, 1)
            act.wait_ge(up_done, 1)
            for d in range(2):
                nc.scalar.activation(m.win_hi[:, d, :], w_stage[:, d, :], ACT.Copy,
                                     scale=w_up[:, d:d + 1]).then_inc(high_done, 1)

        @block.tensor
        def _(pe):
            pe.wait_ge(dt_done, 1)
            for c in range(CPB):
                last = nc.tensor.transpose(dt_ps[:, c, :], dt[:, c * P:(c + 1) * P], m.ident[0:R, 0:R])
            last.then_inc(tables_ready, 1)
            pe.wait_ge(prefix_done, 1)
            for c in range(CPB):
                last = nc.tensor.transpose(pre_ps[:, c, :], prefix[:, c * P:(c + 1) * P], m.ident[0:R, 0:R])
            last.then_inc(tables_ready, 1)
            pe.wait_ge(spread_done, 1)
            nc.tensor.matmul(tot_ps[:], ones[:], spread[:], start=True, stop=True).then_inc(tables_ready, 1)


def run_ssm(nc, m):
    with ExitStack() as ctx:
        def sem(name):
            return ctx.enter_context(nc.semaphore(name))

        def sb(name, shape, dt=F32):
            return ctx.enter_context(nc.sbuf_tensor("ssm_" + name, shape, dt))

        def ps(name, shape, dt=F32):
            return ctx.enter_context(nc.psum_tensor("ssm_" + name, shape, dt))

        TILE = 8
        UPS = 4
        X0, X1, B, C = range(4)
        conv_out = [[sb(f"conv_out{p}{d}", [P, 4, SS]) for d in range(2)] for p in range(2)]
        conv_acc = [sb(f"conv_acc{i}", [P, SS]) for i in range(2)]
        reach = [sb(f"reach{d}", [P, NH, P]) for d in range(2)]
        score = [sb(f"score{d}", [P, NH, P]) for d in range(2)]
        x_dt = [sb(f"x_dt{d}", [P, NH, HD]) for d in range(2)]
        x_end = [sb(f"x_end{d}", [P, NH, HD]) for d in range(2)]
        b_tok = [sb(f"b_tok{d}", [P, DS]) for d in range(2)]
        z_act = [sb(f"z_act{d}", [P, DI]) for d in range(2)]
        carried = [sb(f"carried{d}", [P, NH, HD]) for d in range(2)]
        y_sb = [sb(f"y_sb{d}", [P, DI]) for d in range(2)]
        gated_t = [sb(f"gated_t{d}", [P, 2, P]) for d in range(2)]
        squares = sb("squares", [P, DI])
        mean_sq = [sb(f"mean_sq{d}", [P, 1]) for d in range(2)]
        mean_eps = [sb(f"mean_eps{d}", [P, 1]) for d in range(2)]
        rms = [sb(f"rms{d}", [P, 1]) for d in range(2)]
        warm = sb("warm", [P, 1])

        u_ps = [ps(f"u_ps{i}", [P, SS + NCONV - 1]) for i in range(2)]
        decay_ps = ps("decay_ps", [P, NH, P])
        gx_ps = ps("gx_ps", [P, 3, P])
        bz_ps = ps("bz_ps", [P, 3, P])
        y_ps = ps("y_ps", [P, 2, DI])
        s_ps = ps("s_ps", [P, NH, HD])
        o_ps = ps("o_ps", [P, 3, P])

        names = ("u_ready tap0_done taps_done taps_step xs_done gx_ready decay_ready bz_ready scan_done "
                 "score_done xdt_done xend_done z_done y_ready s_ready carried_done yprev_done y_done "
                 "state_done gated_done square_done eps_done rms_done gt_ready gt_copied out_ready out_done")
        S = {n: sem(n) for n in names.split()}
        block = ctx.enter_context(nc.Block())

        def supersteps(eng, prologue, slot, epilogue):
            prologue()

            def step(f, par):
                s = (f, NSS - 1 - f) if isinstance(f, int) else (f, eng.snap(f * (-1) + (NSS - 1)))
                last = isinstance(f, int) and f == NSS - 1
                for j in range(UPS):
                    slot(s, par, j, last)

            step(0, 0)
            step(1, 1)
            with eng.Fori(1, NSS // 2 - 1) as i:
                for par in range(2):
                    step(2 * i + par, par)
            step(NSS - 2, 0)
            step(NSS - 1, 1)
            epilogue()

        FIRST, LAST = (0, NSS - 1), (NSS - 1, 0)

        def after(s):
            return s[0] + 1, s[1] - 1

        def before(s):
            return s[0] - 1, s[1] + 1

        def chunk_in(j):
            d, c = j % 2, j // 2
            return c if d == 0 else 1 - c

        def chunk_of(eng, s, j):
            chunk = 2 * s[j % 2] + chunk_in(j)
            return chunk if isinstance(chunk, int) else eng.snap(chunk)

        def unit_before(s, par, j, back):
            if j >= back:
                return s, par, j - back
            return before(s), 1 - par, j - back + UPS

        def is_unit(s, j, back):
            return not isinstance(s[0], int) or UPS * s[0] + j >= back

        def next_unit(s, par, j):
            return (s, par, j + 1) if j + 1 < UPS else (after(s), 1 - par, 0)

        def tokens(t, s, d, first, count):
            return t[:, ds(s[d], 1), first:first + count].rearrange("p o t -> p (o t)")

        @block.tensor
        def _(pe):
            MM = nc.tensor.matmul

            def conv_tile(s, i):
                T, d, g = TILE * s[0] + i, i // 4, i % 4
                need(pe, S["taps_done"], T - 1)
                first = HALO - (NCONV - 1) if d == 0 else HALO
                cols = slice(DI + g * P, DI + (g + 1) * P)
                xh, xl = (tokens(t, s, d, first, SS + NCONV - 1) for t in (m.xhi, m.xlo))
                MM(u_ps[i % 2][:], m.win_hi[:, d, cols], xh, start=True, stop=False)
                MM(u_ps[i % 2][:], m.win_hi[:, d, cols], xl, start=False, stop=False)
                MM(u_ps[i % 2][:], m.win_lo[:, d, cols], xh, start=False, stop=True).then_inc(S["u_ready"], 1)

            def front(s, par, j):
                K, d, c = UPS * s[0] + j, j % 2, chunk_in(j)
                xs, at = conv_out[par][d], slice(c * P, (c + 1) * P)
                chunk = chunk_of(pe, s, j)
                need(pe, S["xs_done"], TILE * s[0] + 4 * (d + 1))
                need(pe, S["xdt_done"], K)
                MM(gx_ps[:, 0, :], xs[:, B, at], xs[:, C, at], start=True, stop=True)
                nc.tensor.transpose(gx_ps[:, 1, :], xs[:, X0, at], m.ident[:])
                nc.tensor.transpose(gx_ps[:, 2, :], xs[:, X1, at], m.ident[:]).then_inc(S["gx_ready"], 1)
                need(pe, S["scan_done"], K)
                for h in range(NH):
                    last = MM(decay_ps[:, h, :], m.head_select[:, d, h, :], m.decay_parts[:, ds(chunk * P, P)],
                              start=True, stop=True)
                last.then_inc(S["decay_ready"], 1)
                need(pe, S["z_done"], K)
                nc.tensor.transpose(bz_ps[:, 0, :], xs[:, B, at], m.ident[:])
                zh, zl = (tokens(t, s, d, HALO + c * P, P) for t in (m.xhi, m.xlo))
                z = bz_ps[:, 1:3, :].rearrange("p a b -> p (a b)")
                MM(z, zh, m.win_hi[:, d, 0:DI], start=True, stop=False)
                MM(z, zh, m.win_lo[:, d, 0:DI], start=False, stop=False)
                MM(z, zl, m.win_hi[:, d, 0:DI], start=False, stop=True).then_inc(S["bz_ready"], 1)

            def middle(s, par, j):
                K, d, c = UPS * s[0] + j, j % 2, chunk_in(j)
                xs, at = conv_out[par][d], slice(c * P, (c + 1) * P)
                need(pe, S["y_done"], K)
                for k in range(2):
                    MM(y_ps[:, 0, k * P:(k + 1) * P], xs[:, k, at], m.skip_diag[:, d, k, :],
                       start=(k == 0), stop=False, skip_group_check=True)
                need(pe, S["state_done"], K - 1)
                MM(y_ps[:, 1, :], xs[:, C, at], m.state[:, d, :], start=False, stop=False,
                   skip_group_check=True)
                need(pe, S["xdt_done"], K + 1)
                for h in range(NH):
                    last = MM(y_ps[:, 0, h * HD:(h + 1) * HD], score[d][:, h, :], x_dt[d][:, h, :],
                              start=False, stop=(h == NH - 1), skip_group_check=True)
                last.then_inc(S["y_ready"], 1)
                need(pe, S["xend_done"], K + 1)
                need(pe, S["z_done"], K + 1)
                need(pe, S["state_done"], K)
                MM(s_ps[:], b_tok[d][:], x_end[d][:], start=True, stop=True).then_inc(S["s_ready"], 1)

            def back_a(s, j):
                K, d = UPS * s[0] + j, j % 2
                need(pe, S["gated_done"], K + 1)
                need(pe, S["out_done"], K)
                for k in range(2):
                    last = nc.tensor.transpose(o_ps[:, k, :], y_sb[d][:, k * P:(k + 1) * P], m.ident[:])
                last.then_inc(S["gt_ready"], 1)

            def back_b(s, j):
                K, d = UPS * s[0] + j, j % 2
                need(pe, S["gt_copied"], K + 1)
                for k in range(2):
                    last = MM(o_ps[:, 2, :], gated_t[d][:, k, :], m.w_out[:, d, k, :],
                              start=(k == 0), stop=(k == 1))
                last.then_inc(S["out_ready"], 1)

            def prologue():
                for i in range(TILE):
                    conv_tile(FIRST, i)
                front(FIRST, 0, 0)

            def slot(s, par, j, last):
                if not last:
                    conv_tile(after(s), 2 * j)
                    conv_tile(after(s), 2 * j + 1)
                if not (last and j == UPS - 1):
                    front(*next_unit(s, par, j))
                if is_unit(s, j, 2):
                    s2, _, j2 = unit_before(s, par, j, 2)
                    back_b(s2, j2)
                middle(s, par, j)
                if is_unit(s, j, 1):
                    s1, _, j1 = unit_before(s, par, j, 1)
                    back_a(s1, j1)

            def epilogue():
                back_b(LAST, UPS - 2)
                back_a(LAST, UPS - 1)
                back_b(LAST, UPS - 1)

            supersteps(pe, prologue, slot, epilogue)

        @block.scalar
        def _(act):
            def tap0(s, i):
                T, d, g = TILE * s[0] + i, i // 4, i % 4
                need(act, S["u_ready"], T + 1)
                need(act, S["xs_done"], T - 1)
                at = 0 if d == 0 else NCONV - 1
                nc.scalar.activation(conv_acc[i % 2][:], u_ps[i % 2][:, at:at + SS], ACT.Identity,
                                     bias=m.conv_b[:, d, g:g + 1],
                                     scale=m.conv_w[:, d, g, 0:1]).then_inc(S["tap0_done"], 1)

            def conv_silu(s, par, i):
                T, d, g = TILE * s[0] + i, i // 4, i % 4
                need(act, S["taps_done"], T + 1)
                need(act, S["s_ready"], UPS * (s[0] - 1))
                nc.scalar.activation(conv_out[par][d][:, g, :], conv_acc[i % 2][:],
                                     ACT.Silu).then_inc(S["xs_done"], 1)

            def front(s, j):
                K, d = UPS * s[0] + j, j % 2
                need(act, S["bz_ready"], K + 1)
                need(act, S["s_ready"], K - 1)
                nc.scalar.activation(b_tok[d][:], bz_ps[:, 0, :], ACT.Copy)
                need(act, S["gated_done"], K - 1)
                nc.scalar.activation(z_act[d][:], bz_ps[:, 1:3, :].rearrange("p a b -> p (a b)"), ACT.Silu,
                                     scale=m.in_back[:, d:d + 1]).then_inc(S["z_done"], 1)

            def square(s, j):
                K, d = UPS * s[0] + j, j % 2
                need(act, S["gated_done"], K + 1)
                need(act, S["square_done"], K)
                need(act, S["eps_done"], K - 1)
                nc.scalar.activation(squares[:], y_sb[d][:], ACT.Square, scale=DI ** -0.5,
                                     accum_out=mean_sq[d][:]).then_inc(S["square_done"], 1)

            def copy_t(s, j):
                K, d = UPS * s[0] + j, j % 2
                need(act, S["gt_ready"], K + 1)
                need(act, S["out_ready"], K - 1)
                nc.scalar.activation(gated_t[d][:], o_ps[:, 0:2, :], ACT.Copy).then_inc(S["gt_copied"], 1)

            def out(s, j):
                K, d, chunk = UPS * s[0] + j, j % 2, chunk_of(act, s, j)
                need(act, S["out_ready"], K + 1)
                need(act, S["rms_done"], K + 1)
                nc.scalar.activation(m.out[:, d, ds(chunk, 1), :].rearrange("p o d -> p (o d)"),
                                     o_ps[:, 2, :], ACT.Copy, scale=rms[d][:, 0:1]).then_inc(S["out_done"], 1)

            def prologue():
                nc.scalar.activation(warm[:], m.minus_half[:, 0:1], ACT.Silu)
                for i in range(0, TILE, 2):
                    for k in (i, i + 1):
                        tap0(FIRST, k)
                    for k in (i, i + 1):
                        conv_silu(FIRST, 0, k)
                front(FIRST, 0)

            def slot(s, par, j, last):
                if not last:
                    tap0(after(s), 2 * j)
                    tap0(after(s), 2 * j + 1)
                if not (last and j == UPS - 1):
                    sn, _, jn = next_unit(s, par, j)
                    front(sn, jn)
                if is_unit(s, j, 2):
                    s2, _, j2 = unit_before(s, par, j, 2)
                    out(s2, j2)
                if not last:
                    conv_silu(after(s), 1 - par, 2 * j)
                    conv_silu(after(s), 1 - par, 2 * j + 1)
                if is_unit(s, j, 1):
                    s1, _, j1 = unit_before(s, par, j, 1)
                    square(s1, j1)
                    copy_t(s1, j1)

            def epilogue():
                out(LAST, UPS - 2)
                square(LAST, UPS - 1)
                copy_t(LAST, UPS - 1)
                out(LAST, UPS - 1)

            supersteps(act, prologue, slot, epilogue)

        @block.vector
        def _(dve):
            V = nc.vector

            def taps(s, i0):
                for tap in range(1, NCONV):
                    for i in (i0, i0 + 1):
                        T, d, g = TILE * s[0] + i, i // 4, i % 4
                        if tap == 1:
                            need(dve, S["tap0_done"], T + 1)
                        else:
                            need(dve, S["taps_step"], (TILE * s[0] + i0) * (NCONV - 2) + 2 * (tap - 2) + i - i0 + 1)
                        at = tap if d == 0 else NCONV - 1 - tap
                        V.scalar_tensor_tensor(conv_acc[i % 2][:], u_ps[i % 2][:, at:at + SS],
                                               m.conv_w[:, d, g, tap:tap + 1], conv_acc[i % 2][:],
                                               ALU.mult, ALU.add
                                               ).then_inc(S["taps_done" if tap == NCONV - 1 else "taps_step"], 1)

            def front(s, j):
                K, d, chunk = UPS * s[0] + j, j % 2, chunk_of(dve, s, j)
                flat = [t[:].rearrange("p h t -> p (h t)") for t in (reach[d], decay_ps, m.ident4)]
                if d == 1:
                    flat = [t[:, ::-1] for t in flat]
                need(dve, S["decay_ready"], K + 1)
                need(dve, S["xend_done"], K - 1)
                V.tensor_tensor_scan(flat[0], flat[1], flat[2], 0.0, ALU.mult,
                                     ALU.add).then_inc(S["scan_done"], 1)
                need(dve, S["gx_ready"], K + 1)
                need(dve, S["s_ready"], K - 1)
                V.tensor_tensor(x_dt[d][:], gx_ps[:, 1:3, :].rearrange("p a (h c) -> p (a h) c", c=HD),
                                m.dt_tok[:, d, ds(chunk, 1), :].rearrange("p o h -> p (o h)").unsqueeze(2)
                                .broadcast_to([P, NH, HD]), ALU.mult)
                need(dve, S["scan_done"], K + 1)
                V.tensor_tensor(score[d][:], reach[d][:], gx_ps[:, 0:1, :].broadcast_to([P, NH, P]),
                                ALU.mult).then_inc(S["xdt_done"], 1)

            def middle(s, j):
                K, d, chunk = UPS * s[0] + j, j % 2, chunk_of(dve, s, j)
                need(dve, S["y_ready"], K + 1)
                need(dve, S["gt_ready"], K - 1)
                need(dve, S["square_done"], K - 1)
                V.tensor_tensor(y_sb[d][:].rearrange("p (h c) -> p h c", c=HD), y_ps[:, 1, :].rearrange("p (h c) -> p h c", c=HD),
                                m.prefix_tok[:, d, ds(chunk, 1), :].rearrange("p o h -> p (o h)").unsqueeze(2)
                                .broadcast_to([P, NH, HD]), ALU.mult).then_inc(S["yprev_done"], 1)
                need(dve, S["s_ready"], K + 1)
                need(dve, S["carried_done"], K + 1)
                V.tensor_tensor(m.state[:, d, :], s_ps[:].rearrange("p h c -> p (h c)"),
                                carried[d][:].rearrange("p h c -> p (h c)"), ALU.add
                                ).then_inc(S["state_done"], 1)
                need(dve, S["yprev_done"], K + 1)
                V.tensor_tensor(y_sb[d][:], y_ps[:, 0, :], y_sb[d][:], ALU.add).then_inc(S["y_done"], 1)

            def prologue():
                for i in range(0, TILE, 2):
                    taps(FIRST, i)
                front(FIRST, 0)

            def slot(s, par, j, last):
                if not (last and j == UPS - 1):
                    sn, _, jn = next_unit(s, par, j)
                    front(sn, jn)
                if not last:
                    taps(after(s), 2 * j)
                middle(s, j)

            supersteps(dve, prologue, slot, lambda: None)

        @block.gpsimd
        def _(pool):
            G = nc.gpsimd

            def front(s, j):
                K, d = UPS * s[0] + j, j % 2
                end = P - 1 if d == 0 else 0
                need(pool, S["xdt_done"], K + 1)
                need(pool, S["s_ready"], K - 1)
                G.tensor_tensor(x_end[d][:], x_dt[d][:], reach[d][:, :, end:end + 1].broadcast_to([P, NH, HD]),
                                ALU.mult).then_inc(S["xend_done"], 1)

            def middle(s, j):
                K, d, chunk = UPS * s[0] + j, j % 2, chunk_of(pool, s, j)
                need(pool, S["state_done"], K - 1)
                G.tensor_tensor(carried[d][:], m.state[:, d, :].rearrange("p (h c) -> p h c", c=HD),
                                m.tot[:, d, ds(chunk, 1), :].rearrange("p o h -> p (o h)").unsqueeze(2)
                                .broadcast_to([P, NH, HD]), ALU.mult).then_inc(S["carried_done"], 1)
                need(pool, S["y_done"], K + 1)
                need(pool, S["z_done"], K + 1)
                G.tensor_tensor(y_sb[d][:], y_sb[d][:], z_act[d][:], ALU.mult).then_inc(S["gated_done"], 1)

            def norm(s, j):
                K, d = UPS * s[0] + j, j % 2
                need(pool, S["square_done"], K + 1)
                need(pool, S["rms_done"], K - 1)
                G.tensor_tensor(mean_eps[d][:], mean_sq[d][:], m.eps[:], ALU.add).then_inc(S["eps_done"], 1)
                need(pool, S["eps_done"], K + 1)
                need(pool, S["out_done"], K - 1)
                G.tensor_tensor(rms[d][:], mean_eps[d][:], m.minus_half[:, 0:1],
                                ALU.pow).then_inc(S["rms_done"], 1)

            def prologue():
                front(FIRST, 0)

            def slot(s, par, j, last):
                if not (last and j == UPS - 1):
                    sn, _, jn = next_unit(s, par, j)
                    front(sn, jn)
                middle(s, j)
                if is_unit(s, j, 1):
                    s1, _, j1 = unit_before(s, par, j, 1)
                    norm(s1, j1)

            supersteps(pool, prologue, slot, lambda: norm(LAST, UPS - 1))


def write_out(nc, m):
    with ExitStack() as ctx:
        TPG = 8
        NG = TILES // TPG
        x_sb = [ctx.enter_context(nc.sbuf_tensor(f"x_res{k}", [P, TPG, DM], F32)) for k in range(2)]
        both = [ctx.enter_context(nc.sbuf_tensor(f"both{k}", [P, TPG, DM], F32)) for k in range(2)]
        res = [ctx.enter_context(nc.sbuf_tensor(f"res{k}", [P, TPG, DM], F32)) for k in range(2)]
        loaded = [ctx.enter_context(nc.semaphore(f"x_loaded{k}")) for k in range(2)]
        summed = ctx.enter_context(nc.semaphore("summed"))
        scaled = ctx.enter_context(nc.semaphore("scaled"))
        added = ctx.enter_context(nc.semaphore("added"))
        stored = [ctx.enter_context(nc.semaphore(f"stored{k}")) for k in range(2)]
        block = ctx.enter_context(nc.Block())

        def tiles(t, g):
            return t[:, TPG * g:TPG * (g + 1), :]

        @block.sync
        def _(sp):
            for g in range(NG):
                if g >= 2:
                    sp.wait_ge(added, g - 1)
                sp.dma_start(x_sb[g % 2][:], m.dram.x_tiles[:, TPG * g:TPG * (g + 1), :]
                             ).then_inc(loaded[g % 2], 16)

        @block.vector
        def _(dve):
            for g in range(NG):
                if g >= 2:
                    dve.wait_ge(added, g - 1)
                nc.vector.tensor_tensor(both[g % 2][:], tiles(m.out[:, 0], g), tiles(m.out[:, 1], g),
                                        ALU.add).then_inc(summed, 1)
                dve.wait_ge(summed, g + 1)
                nc.vector.tensor_tensor(both[g % 2][:], both[g % 2][:], tiles(m.gate, g),
                                        ALU.mult).then_inc(scaled, 1)

        @block.gpsimd
        def _(pool):
            for g in range(NG):
                pool.wait_ge(scaled, g + 1)
                pool.wait_ge(loaded[g % 2], 16 * (g // 2 + 1))
                if g >= 2:
                    pool.wait_ge(stored[g % 2], 16 * (g // 2))
                nc.gpsimd.tensor_tensor(res[g % 2][:], both[g % 2][:], x_sb[g % 2][:], ALU.add).then_inc(added, 1)

        @block.scalar
        def _(act):
            for g in range(NG):
                act.wait_ge(added, g + 1)
                act.dma_start(m.dram.out_tiles[:, TPG * g:TPG * (g + 1), :], res[g % 2][:]
                              ).then_inc(stored[g % 2], 16)
            for k in range(2):
                act.wait_ge(stored[k], 16 * (NG // 2))


def build(nc, ins, outs):
    m, d = Memory(), Memory()
    m.dram = d
    d.x_blocks = ins["x"].rearrange("b t d -> (b t) d").rearrange("(n j p) d -> n p j d", p=P, j=TPB)
    d.w_gate, d.w_down = ins["w_gate"], ins["w_down"]
    d.w_gate_shared, d.w_down_shared = ins["w_gate_shared"], ins["w_down_shared"]
    d.router = ins["router"]
    d.expert_bias = ins["expert_bias"].rearrange("(o e) -> o e", o=1).to_broadcast([P, NE])
    d.w_in = [ins["w_in_f"], ins["w_in_b"]]
    d.dt_bias, d.a_log, d.conv_w, d.conv_b = ins["dt_bias"], ins["a_log"], ins["conv_w"], ins["conv_b"]
    d.skip, d.norm_w, d.w_out = ins["skip"], ins["norm_w"], ins["w_out"]
    flat = "b t d -> (b t) d"
    d.x_tiles = ins["x"].rearrange(flat).rearrange("(n p) d -> p n d", p=P)
    d.out_tiles = outs["out"].rearrange(flat).rearrange("(n p) d -> p n d", p=P)
    d.comb_scratch = nc.dram_tensor("comb_scratch", [NBLK, 2 * EQ, NQ, BLK], F16, kind="Internal").ap()
    d.dt_scratch = nc.dram_tensor("dt_scratch", [NBLK, 36, BLK], F32, kind="Internal").ap()
    d.decay_scratch = nc.dram_tensor("decay_scratch", [3, 2 * NH * BATCH, SEQ], BF16, kind="Internal").ap()
    with ExitStack() as ctx:
        def sb(name, shape, dt=F32):
            return ctx.enter_context(nc.sbuf_tensor(name, shape, dt))

        m.experts = sb("experts", [P, 2 * NE * INTER])
        w16 = m.experts[:].bitcast(F16).rearrange("p (k n) -> p k n", k=4)
        m.wg_hi, m.wg_lo, m.wd_hi, m.wd_lo = (w16[:, k, :] for k in range(4))
        m.gate = sb("gate", [P, TILES, DM])
        m.xhi, m.xlo = sb("xhi", [P, NSS, SW], F16), sb("xlo", [P, NSS, SW], F16)
        m.gate_back, m.moe_back, m.kappa = sb("gate_back", [P, 1]), sb("moe_back", [P, 1]), sb("kappa", [P, 1])
        m.ident, m.minus_half, m.eps = sb("ident", [P, P]), sb("minus_half", [P, TPB]), sb("eps", [P, 1])
        with (nc.sbuf_tensor("sh_hi", [P, 2, P], F16) as m.sh_hi, nc.sbuf_tensor("sh_lo", [P, 2, P], F16) as m.sh_lo,
              nc.sbuf_tensor("pair_select", [2 * EQ, EQ * INTER], F16) as m.pair_select,
              nc.sbuf_tensor("ident16", [P, P], F16) as m.ident16):
            scale_weights(nc, m)
            prepare_tokens(nc, m)
            run_experts(nc, m)
        m.out = m.experts[:, 0:2 * TILES * DM].rearrange("p (d n c) -> p d n c", d=2, n=TILES)
        m.decay_parts = m.experts[0:6 * NH, 2 * TILES * DM:].bitcast(BF16)
        m.state = sb("state", [P, 2, DI])
        m.win_hi, m.win_lo = sb("win_hi", [P, 2, 3 * DI], F16), sb("win_lo", [P, 2, 3 * DI], F16)
        m.in_back = sb("in_back", [P, 2])
        m.conv_w, m.conv_b = sb("conv_w", [P, 2, 4, NCONV]), sb("conv_b", [P, 2, 4])
        m.skip_diag = sb("skip_diag", [P, 2, 2, P])
        m.w_out = sb("w_out", [P, 2, 2, DM])
        m.ident4 = sb("ident4", [P, NH, P], BF16)
        m.head_select = sb("head_select", [6 * NH, 2, NH, P], BF16)
        m.tot, m.dt_tok, m.prefix_tok = (sb(n, [P, 2, TILES, NH]) for n in ("tot_all", "dt_tok", "prefix_tok"))
        prepare_decays(nc, m)
        run_ssm(nc, m)
        write_out(nc, m)


def kernel_inputs(inputs):
    g = {k: np.asarray(v) for k, v in inputs.items()}
    c = np.ascontiguousarray
    a = {"x": g["L0_attn_u"], "expert_bias": g["L0_ffn_expert_bias"]}
    a["w_gate"] = c(g["L0_ffn_w_gate"].reshape(NE * INTER, DM).T)
    a["w_down"] = c(g["L0_ffn_w_down"].transpose(0, 2, 1).reshape(NE // 2, P, DM).transpose(1, 0, 2)
                    .reshape(P, NE * INTER))
    a["w_gate_shared"] = c(g["L0_ffn_w_gate_shared"].T)
    a["w_down_shared"] = c(g["L0_ffn_w_down_shared"].T)
    a["router"] = c(g["L0_ffn_router_w"].T)
    both = {k: [g[f"L0_attn_{k}_{s}"] for s in "fb"]
            for k in ("Wi", "conv_w", "conv_b", "dt_bias", "A_log", "D", "norm_w", "Wo")}
    a["w_in_f"], a["w_in_b"] = (c(w.T) for w in both["Wi"])
    a["dt_bias"] = np.repeat(np.concatenate(both["dt_bias"]), BATCH).reshape(-1, 1)
    a["a_log"] = np.repeat(np.concatenate(both["A_log"]), BATCH).reshape(-1, 1)
    a["conv_w"] = c(np.stack(both["conv_w"]).reshape(2, 4, P, NCONV).transpose(2, 0, 1, 3))
    a["conv_b"] = c(np.stack(both["conv_b"]).reshape(2, 4, P).transpose(2, 0, 1))
    a["skip"] = c(np.repeat(np.stack(both["D"]), HD, axis=1).reshape(2, 2, P).transpose(2, 0, 1))
    a["norm_w"] = c(np.stack(both["norm_w"]).reshape(2, 2, P).transpose(2, 0, 1))
    a["w_out"] = c(np.stack([w.T for w in both["Wo"]]).reshape(2, 2, P, DM).transpose(2, 0, 1, 3))
    return a


def kernel(**inputs):
    import concourse.bacc as _bacc
    from concourse.bass_utils import run_bass_kernel_spmd as _run

    nc = _bacc.Bacc("TRN2", target_bir_lowering=False, num_devices=1)
    arrays, ins = {}, {}
    for name, a in kernel_inputs(inputs).items():
        a = np.ascontiguousarray(a)
        arrays[f"in_{name}_dram"] = a
        ins[name] = nc.dram_tensor(f"in_{name}_dram", a.shape, mybir.dt.from_np(a.dtype), kind="ExternalInput").ap()
    out = nc.dram_tensor("out_0_dram", (BATCH, SEQ, DM), F32, kind="ExternalOutput").ap()
    build(nc, ins, {"out": out})
    r = _run(nc, [arrays], core_ids=[0])
    return r.results[0]["out_0_dram"]
```

```python
from contextlib import ExitStack

import numpy as np
import concourse.bass as bass
from concourse import mybir

F32, F16, BF16, I32 = mybir.dt.float32, mybir.dt.float16, mybir.dt.bfloat16, mybir.dt.int32
ALU = mybir.AluOpType
ACT = mybir.ActivationFunctionType
AX = mybir.AxisListType
ds = bass.ds

P = 128
BATCH, SEQ, DM = 8, 1024, 128
TOKENS = BATCH * SEQ
TILES = TOKENS // P
BLK = 512
NBLK = TOKENS // BLK
TPB = BLK // P
SS = 256
NSS = TOKENS // SS
HALO = 4
SW = SS + 2 * HALO
NE, INTER = 160, 64
NQ = 4
EQ = NE // NQ
NIT = EQ // 2
UNITS = NQ * NIT + 1
NH, HD, DS, DI = 4, 64, 128, 256
NCONV = 4
XSCALE = 64.0
WTOP = 1024.0
RMAX = bass.bass_isa.ReduceOp.max


class Memory:
    pass


def need(eng, sem, count):
    if not isinstance(count, int) or count > 0:
        eng.wait_ge(sem, count)


def scale_weights(nc, m):
    with ExitStack() as ctx:
        def sem(name):
            return ctx.enter_context(nc.semaphore(name))

        NCH, CH = 4, NE * INTER // 4
        wstage = ctx.enter_context(nc.sbuf_tensor("wstage", [P, NE * INTER], F32))
        shared = ctx.enter_context(nc.sbuf_tensor("shared", [P, 2, P], F32))
        part_max = ctx.enter_context(nc.sbuf_tensor("part_max", [P, 2, NCH + 2], F32))
        row_max = ctx.enter_context(nc.sbuf_tensor("row_max", [P, 2], F32))
        all_max = ctx.enter_context(nc.sbuf_tensor("all_max", [P, 2], F32))
        pow2 = ctx.enter_context(nc.sbuf_tensor("pow2", [P, 2], F32))
        up = ctx.enter_context(nc.sbuf_tensor("up", [P, 2], F32))
        loaded = [sem(f"wchunk_loaded{c}") for c in range(NCH)]
        shared_loaded = sem("shared_loaded")
        shared_zero = sem("shared_zero")
        maxed = sem("row_max_done")
        reduced = sem("all_max_done")
        scaled = sem("scales_done")
        high_done = sem("high_done")
        low_done = sem("low_done")
        step = sem("vector_step")
        pool_step = sem("pool_step")
        hi = [m.wg_hi, m.wd_hi]
        lo = [m.wg_lo, m.wd_lo]
        src = [m.dram.w_gate, m.dram.w_down]
        block = ctx.enter_context(nc.Block())

        def chunk(c):
            return slice(c * CH, (c + 1) * CH)

        @block.sync
        def _(sp):
            sp.wait_ge(shared_zero, 1)
            sp.dma_start(shared[:, 0, 0:INTER], m.dram.w_gate_shared).then_inc(shared_loaded, 16)
            sp.dma_start(shared[0:INTER, 1, :], m.dram.w_down_shared).then_inc(shared_loaded, 16)
            for w in range(2):
                for c in range(NCH):
                    if w == 1:
                        sp.wait_ge(low_done, c + 1)
                    sp.dma_start(wstage[:, chunk(c)], src[w][:, chunk(c)]).then_inc(loaded[c], 16)

        @block.vector
        def _(dve):
            n = [0]

            def link(ins):
                n[0] += 1
                ins.then_inc(step, 1)
                dve.wait_ge(step, n[0])

            nc.vector.memset(shared[:], 0.0).then_inc(shared_zero, 1)
            link(nc.vector.memset(part_max[:, :, NCH + 1:], 1e-30))
            dve.wait_ge(shared_loaded, 32)
            for w in range(2):
                nc.vector.tensor_reduce(part_max[:, w, NCH:NCH + 1], shared[:, w, :], AX.X, ALU.max,
                                        apply_absolute_value=True)
            for w in range(2):
                for c in range(NCH):
                    dve.wait_ge(loaded[c], 16 * (w + 1))
                    last = nc.vector.tensor_reduce(part_max[:, w, c:c + 1], wstage[:, chunk(c)], AX.X, ALU.max,
                                                   apply_absolute_value=True)
                link(last)
                nc.vector.tensor_reduce(row_max[:, w:w + 1], part_max[:, w, :], AX.X,
                                        ALU.max).then_inc(maxed, 1)
                dve.wait_ge(reduced, w + 1)
                link(nc.vector.tensor_scalar(pow2[:, w:w + 1].bitcast(I32), all_max[:, w:w + 1].bitcast(I32),
                                             0x7F800000, None, ALU.bitwise_and))
                link(nc.vector.reciprocal(up[:, w:w + 1], pow2[:, w:w + 1]))
                link(nc.vector.tensor_scalar(up[:, w:w + 1], up[:, w:w + 1], WTOP, None, ALU.mult))
                if w == 0:
                    nc.vector.tensor_scalar(m.gate_back[:], pow2[:, 0:1], 1.0 / (XSCALE * WTOP), None, ALU.mult)
                    link(nc.vector.reciprocal(m.kappa[:], pow2[:, 0:1]))
                    nc.vector.tensor_scalar(m.kappa[:], m.kappa[:], 64.0, None,
                                            ALU.mult).then_inc(scaled, 1)
                else:
                    nc.vector.tensor_tensor(m.moe_back[:], pow2[:, 0:1], pow2[:, 1:2],
                                            ALU.mult).then_inc(scaled, 1)
                for c in range(NCH):
                    dve.wait_ge(high_done, w * (NCH + 1) + c + 1)
                    nc.vector.scalar_tensor_tensor(lo[w][:, chunk(c)], wstage[:, chunk(c)], up[:, w:w + 1],
                                                   hi[w][:, chunk(c)], ALU.mult,
                                                   ALU.subtract).then_inc(low_done, 1)
                dve.wait_ge(high_done, (w + 1) * (NCH + 1))
                nc.vector.scalar_tensor_tensor(m.sh_lo[:, w, :], shared[:, w, :], up[:, w:w + 1],
                                               m.sh_hi[:, w, :], ALU.mult, ALU.subtract)
            dve.wait_ge(scaled, 2)
            nc.vector.tensor_scalar(m.moe_back[:], m.moe_back[:], 1.0 / (64.0 * WTOP), None, ALU.mult)

        @block.gpsimd
        def _(pool):
            sel = m.pair_select[:].rearrange("p (e j) -> p e j", j=INTER)
            nc.gpsimd.memset(m.pair_select[:], 0.0).then_inc(pool_step, 1)
            pool.wait_ge(pool_step, 1)
            for k, first in enumerate((0, EQ)):
                nc.gpsimd.affine_select(out=sel, in_=sel, compare_op=ALU.not_equal, fill=1.0, base=-first,
                                        pattern=[[-1, EQ], [0, INTER]],
                                        channel_multiplier=1).then_inc(pool_step, 1)
                pool.wait_ge(pool_step, k + 2)
            nc.gpsimd.memset(m.ident[:], 0.0).then_inc(pool_step, 1)
            pool.wait_ge(pool_step, 4)
            nc.gpsimd.affine_select(out=m.ident[:], in_=m.ident[:], compare_op=ALU.not_equal, fill=1.0, base=0,
                                    pattern=[[-1, P]], channel_multiplier=1).then_inc(pool_step, 1)
            pool.wait_ge(pool_step, 5)
            nc.gpsimd.tensor_copy(m.ident16[:], m.ident[:])
            nc.gpsimd.memset(m.minus_half[:], -0.5)
            nc.gpsimd.memset(m.eps[:], 1e-5)
            for t in (m.xhi, m.xlo):
                for b in range(BATCH):
                    nc.gpsimd.memset(t[:, 4 * b, 0:HALO], 0.0)
                    nc.gpsimd.memset(t[:, 4 * b + 3, SW - HALO:SW], 0.0)
            for w in range(2):
                pool.wait_ge(maxed, w + 1)
                nc.gpsimd.partition_all_reduce(all_max[:, w:w + 1], row_max[:, w:w + 1], P,
                                               RMAX).then_inc(reduced, 1)

        @block.scalar
        def _(act):
            for w in range(2):
                act.wait_ge(scaled, w + 1)
                for c in range(NCH):
                    nc.scalar.activation(hi[w][:, chunk(c)], wstage[:, chunk(c)], ACT.Copy,
                                         scale=up[:, w:w + 1]).then_inc(high_done, 1)
                nc.scalar.activation(m.sh_hi[:, w, :], shared[:, w, :], ACT.Copy,
                                     scale=up[:, w:w + 1]).then_inc(high_done, 1)


def run_experts(nc, m):
    with ExitStack() as ctx:
        def sem(name):
            return ctx.enter_context(nc.semaphore(name))

        def sb(name, shape, dt=F32):
            return ctx.enter_context(nc.sbuf_tensor("moe_" + name, shape, dt))

        def ps(name, shape, dt=F32):
            return ctx.enter_context(nc.psum_tensor("moe_" + name, shape, dt))

        comb_t = sb("comb_t", [2 * EQ, 2, NQ, BLK], F16)
        act_out = [sb(f"silu{k}", [P, BLK]) for k in range(2)]
        prod = [sb(f"prod{k}", [P, BLK]) for k in range(2)]
        h_hi = [sb(f"h_hi{q}", [P, BLK], F16) for q in range(NQ)]
        h_lo = [sb(f"h_lo{q}", [P, BLK], F16) for q in range(NQ)]
        hs_hi = sb("hs_hi", [INTER, BLK], F16)
        hs_lo = sb("hs_lo", [INTER, BLK], F16)
        gate_t = sb("gate_t", [P, BLK])
        x_sb = sb("x_sb", [P, TPB, DM])
        stats = sb("stats", [P, TPB, 6])
        mv = sb("mv", [P, TPB, 2])
        var_eps = sb("var_eps", [P, TPB])
        rstd = sb("rstd", [P, TPB])
        xn = sb("xn", [P, TPB, DM])
        xt = sb("xt", [P, BLK])
        router = sb("router", [P, NE])
        w_dt = sb("w_dt", [P, 36])
        bias = sb("bias", [P, 2, NE])
        logits = sb("logits", [P, TPB, NE])
        probs = sb("probs", [P, TPB, NE])
        top8 = sb("top8", [P, TPB, 8])
        rest = sb("rest", [P, TPB, NE])
        picked = sb("picked", [P, TPB, NE])
        wsum = sb("wsum", [P, TPB])
        wnorm = sb("wnorm", [P, TPB])
        comb = sb("comb", [P, TPB, NE])
        parts = sb("parts", [P, TPB, NQ, 2, EQ], F16)
        dt_raw = sb("dt_raw", [36, BLK])
        up_ps = [ps(f"up_ps{k}", [P, BLK]) for k in range(2)]
        spread_ps = [ps(f"spread_ps{k}", [P, BLK]) for k in range(2)]
        sum_ps = [ps(f"sum_ps{k}", [P, BLK]) for k in range(2)]
        bank_a, bank_b = (ps(n, [P, BLK]) for n in ("bank_a", "bank_b"))
        xt_ps = bank_a
        logit_ps = [t[:, 0:2 * NE].rearrange("p (j e) -> p j e", e=NE) for t in (bank_b, bank_a)]
        dt_ps = bank_b[0:36, :]
        comb_ps = [t[:].bitcast(F16)[0:2 * EQ, :].rearrange("p (q t) -> p q t", q=2) for t in (bank_a, bank_b)]
        back_ps = bank_b[:].rearrange("p (j d) -> p j d", d=DM)

        params = sem("params_loaded")
        w_dt_zero = sem("w_dt_zero")
        step = sem("vector_step")
        apart = sem("apart")
        x_loaded = sem("x_loaded")
        var_done = sem("var_done")
        rstd_done = sem("rstd_done")
        xn_done = sem("xn_done")
        xt_ready = sem("xt_ready")
        xt_copied = sem("xt_copied")
        xhi_done = sem("xhi_done")
        xlo_done = sem("xlo_done")
        logits_ready = sem("logits_ready")
        logits_done = sem("logits_done")
        dt_ready = sem("dt_ready")
        dt_copied = sem("dt_copied")
        dt_stored = sem("dt_stored")
        probs_done = sem("probs_done")
        comb_done = sem("comb_done")
        comb_hi_done = sem("comb_hi_done")
        parts_done = sem("parts_done")
        comb_t_ready = sem("comb_t_ready")
        comb_a_done = sem("comb_a_done")
        comb_b_done = sem("comb_b_done")
        up_done = sem("up_done")
        spread_done = sem("spread_done")
        silu_done = sem("silu_done")
        prod_done = sem("prod_done")
        hi_done = sem("hi_done")
        lo_done = sem("lo_done")
        down_done = sem("down_done")
        gate_t_done = sem("gate_t_done")
        back_ready = sem("back_ready")
        back_copied = sem("back_copied")
        block = ctx.enter_context(nc.Block())

        SH = "shared"

        def blocks(eng, body):
            body(0, 0, True)
            with eng.Fori(0, (NBLK - 2) // 2) as i:
                for h in range(2):
                    body(2 * i + 1 + h, (1 + h) % 2, False)
            body(NBLK - 1, (NBLK - 1) % 2, False)

        def parity(bp, q):
            return (bp + 1 + q) % 2

        NPARAM = 16 * 5
        SLOTS = 10
        LINKS = 8

        def slots_of(prepare, b, bp):
            if isinstance(b, int) and b == NBLK - 1:
                return None
            return lambda k: prepare(b + 1, 1 - bp, k)

        def units_with_slots(eng, turn, slot):
            if slot is None:
                with eng.Fori(1, NIT) as it:
                    turn(it)
                return
            for k in range(SLOTS):
                slot(k)
                with eng.Fori(1 + 2 * k, min(3 + 2 * k, NIT)) as it:
                    turn(it)

        def tokens_of(t, n):
            return t[:, ds(2 * n, 2), HALO:HALO + SS]

        @block.sync
        def _(sp):
            sp.wait_ge(w_dt_zero, 1)
            sp.dma_start(x_sb[:], m.dram.x_blocks[0]).then_inc(x_loaded, 16)
            sp.dma_start(router[:], m.dram.router).then_inc(params, 16)
            for d in range(2):
                sp.dma_start(w_dt[:, 32 * d:32 * d + NH], m.dram.w_in[d][:, 3 * DI:]).then_inc(params, 16)
            for k in range(2):
                sp.dma_start(bias[:, k, :], m.dram.expert_bias).then_inc(params, 16)

            def store_dt(n):
                sp.wait_ge(dt_copied, n + 1)
                sp.dma_start(m.dram.dt_scratch[ds(n, 1)].rearrange("o r t -> (o r) t"), dt_raw[:]
                             ).then_inc(dt_stored, 16)

            with sp.Fori(1, NBLK) as n:
                sp.wait_ge(xn_done, n)
                sp.dma_start(x_sb[:], m.dram.x_blocks[ds(n, 1)].rearrange("o p j d -> p (o j) d")
                             ).then_inc(x_loaded, 16)
                store_dt(n - 1)
            store_dt(NBLK - 1)
            sp.wait_ge(dt_stored, 16 * NBLK)

        @block.tensor
        def _(pe):
            def prepare(n, half, k):
                if k == 2:
                    pe.wait_ge(xn_done, n + 1)
                    need(pe, comb_a_done, n)
                    for j in range(TPB):
                        last = nc.tensor.transpose(xt_ps[:, j * P:(j + 1) * P], xn[:, j, :], m.ident[:])
                    last.then_inc(xt_ready, 1)
                if k == 3 or k == 4:
                    pe.wait_ge(xt_copied, n + 1)
                    if k == 3:
                        need(pe, comb_b_done, n)
                        need(pe, back_copied, n - 1)
                    else:
                        pe.wait_ge(xlo_done, n + 1)
                    for j in range(2):
                        at = (2 * (k - 3) + j) * P
                        last = nc.tensor.matmul(logit_ps[k - 3][:, j, :], xt[:, at:at + P], router[:],
                                                start=True, stop=True)
                    last.then_inc(logits_ready, 1)
                if k == 5:
                    pe.wait_ge(logits_done, 2 * n + 1)
                    nc.tensor.matmul(dt_ps, w_dt[:], xt[:], start=True, stop=True).then_inc(dt_ready, 1)
                if k == 9:
                    pe.wait_ge(parts_done, n + 1)
                    pe.wait_ge(logits_done, 2 * n + 2)
                    pe.wait_ge(dt_copied, n + 1)
                    for h in range(2):
                        for q in (2 * h, 2 * h + 1):
                            for j in range(TPB):
                                last = nc.tensor.transpose(
                                    comb_ps[h][:, q % 2, j * P:(j + 1) * P],
                                    parts[:, j, q].rearrange("p a e -> p (a e)"), m.ident16[:])
                        last.then_inc(comb_t_ready, 1)

            def up(b, bp, K, k, wh, wl, rows=P):
                if K is not None:
                    pe.wait_ge(silu_done, K - 1)
                out = up_ps[k][0:rows].rearrange("p (s t) -> p s t", t=SS)
                nc.tensor.matmul(out, wh, tokens_of(m.xhi, b), start=True, stop=False)
                nc.tensor.matmul(out, wh, tokens_of(m.xlo, b), start=False, stop=False)
                nc.tensor.matmul(out, wl, tokens_of(m.xhi, b), start=False, stop=True).then_inc(up_done, 1)

            def up_unit(b, bp, it, q):
                K = UNITS * b + 1 + NQ * it + q
                at = (NIT * q + it) * P
                early = isinstance(b, int) and isinstance(it, int) and K < 2
                up(b, bp, None if early else K, parity(bp, q), m.wg_hi[:, ds(at, P)], m.wg_lo[:, ds(at, P)])
                if not early:
                    pe.wait_ge(prod_done, K - 1)
                nc.tensor.matmul(spread_ps[q % 2][:], m.pair_select[:, ds(it * P, P)], comb_t[:, bp, q, :],
                                 start=True, stop=True).then_inc(spread_done, 1)

            def down(bp, K, wh, wl, hh, hl, start, stop):
                pe.wait_ge(lo_done, K + 1)
                nc.tensor.matmul(sum_ps[bp][:], wh, hh, start=start, stop=False)
                nc.tensor.matmul(sum_ps[bp][:], wh, hl, start=False, stop=False)
                nc.tensor.matmul(sum_ps[bp][:], wl, hh, start=False,
                                 stop=stop).then_inc(down_done, 1)

            def down_unit(b, bp, it, q, stop=False):
                at = (NIT * q + it) * P
                down(bp, UNITS * b + 1 + NQ * it + q, m.wd_hi[:, ds(at, P)], m.wd_lo[:, ds(at, P)],
                     h_hi[q][:], h_lo[q][:], False, stop)

            def to_tokens(n):
                pe.wait_ge(gate_t_done, n + 2)
                pe.wait_ge(back_copied, n + 1)
                pe.wait_ge(comb_b_done, min(n + 3, NBLK) if isinstance(n, int) else n + 3)
                for j in range(TPB):
                    last = nc.tensor.transpose(back_ps[:, j, :], gate_t[:, j * P:(j + 1) * P], m.ident[:])
                last.then_inc(back_ready, 1)

            def body(b, bp, first):
                K = UNITS * b
                pe.wait_ge(xlo_done, b + 1)
                pe.wait_ge(comb_a_done, b + 1)
                pe.wait_ge(comb_b_done, b + 1)
                up(b, bp, None if first else K, bp, m.sh_hi[:, 0, 0:INTER], m.sh_lo[:, 0, 0:INTER], rows=INTER)
                for q in range(NQ):
                    up_unit(b, bp, 0, q)
                    if not first:
                        down_unit(b - 1, 1 - bp, NIT - 1, q, stop=q == NQ - 1)
                if not first:
                    pe.wait_ge(gate_t_done, b)
                down(bp, K, m.sh_hi[0:INTER, 1, :], m.sh_lo[0:INTER, 1, :], hs_hi[:], hs_lo[:], True, False)

                def turn(it):
                    for q in range(NQ):
                        up_unit(b, bp, it, q)
                        down_unit(b, bp, it - 1, q)

                units_with_slots(pe, turn, slots_of(prepare, b, bp))
                if not first:
                    to_tokens(b - 1)

            pe.sem_inc(back_ready, 1)
            pe.wait_ge(params, NPARAM)
            for k in range(SLOTS):
                prepare(0, 0, k)
            blocks(pe, body)
            b, bp = NBLK - 1, (NBLK - 1) % 2
            for q in range(NQ):
                down_unit(b, bp, NIT - 1, q, stop=q == NQ - 1)
            to_tokens(b)

        @block.scalar
        def _(act):
            def prepare(n, half, k):
                if k == 2:
                    act.wait_ge(xt_ready, n + 1)
                    need(act, dt_ready, n)
                    nc.scalar.activation(xt[:], xt_ps[:], ACT.Copy).then_inc(xt_copied, 1)
                    nc.scalar.activation(tokens_of(m.xhi, n), xt_ps[:].rearrange("p (s t) -> p s t", t=SS),
                                         ACT.Copy, scale=XSCALE).then_inc(xhi_done, 1)
                if k == 5:
                    act.wait_ge(logits_done, 2 * n + 2)
                    nc.scalar.activation(probs[:], logits[:], ACT.Sigmoid).then_inc(probs_done, 1)
                    act.wait_ge(dt_ready, n + 1)
                    need(act, dt_stored, 16 * n)
                    nc.scalar.activation(dt_raw[:], dt_ps, ACT.Copy).then_inc(dt_copied, 1)
                if k == 8:
                    act.wait_ge(comb_done, n + 1)
                    need(act, comb_t_ready, 2 * n)
                    nc.scalar.activation(parts[:, :, :, 0, :], comb[:].rearrange("p j (q e) -> p j q e", q=NQ),
                                         ACT.Copy).then_inc(comb_hi_done, 1)
                if k == 9:
                    act.wait_ge(comb_t_ready, 2 * n + 1)
                    nc.scalar.activation(comb_t[:, half, 0:2, :], comb_ps[0], ACT.Copy).then_inc(comb_a_done, 1)

            def silu(K, k, rows=P, early=False):
                act.wait_ge(up_done, K + 1)
                if not early:
                    act.wait_ge(prod_done, K - 1)
                nc.scalar.activation(act_out[k][0:rows], up_ps[k][0:rows], ACT.Silu,
                                     scale=m.gate_back[0:rows, 0:1]).then_inc(silu_done, 1)

            def high(K, k, out, rows, free):
                act.wait_ge(prod_done, K + 1)
                if free is not None:
                    act.wait_ge(down_done, free)
                nc.scalar.activation(out[0:rows], prod[k][0:rows], ACT.Copy).then_inc(hi_done, 1)

            def gate(b, bp):
                act.wait_ge(down_done, UNITS * (b + 1))
                act.wait_ge(back_ready, b + 1)
                nc.scalar.activation(gate_t[:], sum_ps[bp][:], ACT.Silu,
                                     scale=m.moe_back[:, 0:1]).then_inc(gate_t_done, 1)

            def body(b, bp, first):
                K = UNITS * b
                silu(K, bp, INTER, early=first)
                if not first:
                    high(K - 1, parity(1 - bp, NQ - 1), h_hi[NQ - 1], P, K - 1 - NQ + 1)
                for q in range(NQ):
                    silu(K + 1 + q, parity(bp, q), early=first and q == 0)
                    if q == 0:
                        high(K, bp, hs_hi, INTER, None if first else K - UNITS + 1)
                    else:
                        high(K + q, parity(bp, q - 1), h_hi[q - 1], P, None if first else K - NQ + q)
                if not first:
                    gate(b - 1, 1 - bp)

                def turn(it):
                    for q in range(NQ):
                        k = K + 1 + NQ * it + q
                        silu(k, parity(bp, q))
                        if q == 0:
                            prev_free(b, bp, it, k)
                        else:
                            high(k - 1, parity(bp, q - 1), h_hi[q - 1], P, k - 1 - NQ + 1)

                units_with_slots(act, turn, slots_of(prepare, b, bp))

            def prev_free(b, bp, it, k):
                high(k - 1, parity(bp, NQ - 1), h_hi[NQ - 1], P, k - 1 - NQ + 1)

            act.sem_inc(gate_t_done, 1)
            for k in range(SLOTS):
                prepare(0, 0, k)
            blocks(act, body)
            b, bp = NBLK - 1, (NBLK - 1) % 2
            K = UNITS * (b + 1)
            high(K - 1, parity(bp, NQ - 1), h_hi[NQ - 1], P, K - 1 - NQ + 1)
            gate(b, bp)

        @block.gpsimd
        def _(pool):
            def prepare(n, half, k):
                if k == 0:
                    pool.wait_ge(var_done, n + 1)
                    nc.gpsimd.tensor_tensor(rstd[:], var_eps[:], m.minus_half[:, 0:TPB],
                                            ALU.pow).then_inc(rstd_done, 1)
                if k == 4:
                    pool.wait_ge(xhi_done, n + 1)
                    pool.wait_ge(xlo_done, n + 1)
                    for t in (m.xhi, m.xlo):
                        left, right = t[:, ds(2 * n, 1)], t[:, ds(2 * n + 1, 1)]
                        nc.gpsimd.tensor_copy(left[:, :, HALO + SS:], right[:, :, HALO:2 * HALO])
                        nc.gpsimd.tensor_copy(right[:, :, 0:HALO], left[:, :, SS:SS + HALO])
                        if half == 0:
                            nxt = t[:, ds(2 * n + 2, 1)]
                            nc.gpsimd.tensor_copy(nxt[:, :, 0:HALO], right[:, :, SS:SS + HALO])
                        else:
                            prev = t[:, ds(2 * n - 1, 1)]
                            nc.gpsimd.tensor_copy(prev[:, :, HALO + SS:], left[:, :, HALO:2 * HALO])

            def low(K, k, out, high, rows=P):
                pool.wait_ge(hi_done, K + 1)
                nc.gpsimd.tensor_tensor(out[0:rows], prod[k][0:rows], high[0:rows],
                                        ALU.subtract).then_inc(lo_done, 1)

            def body(b, bp, first):
                K = UNITS * b
                low(K, bp, hs_lo, hs_hi, INTER)

                def turn(it):
                    for q in range(NQ):
                        low(K + 1 + NQ * it + q, parity(bp, q), h_lo[q], h_hi[q])

                turn(0)
                units_with_slots(pool, turn, slots_of(prepare, b, bp))

            for k in range(SLOTS):
                prepare(0, 0, k)
            blocks(pool, body)

        @block.vector
        def _(dve):
            def prepare(n, half, k):
                def link(ins, number):
                    ins.then_inc(step, 1)
                    dve.wait_ge(step, LINKS * n + number)

                if k == 0:
                    dve.wait_ge(x_loaded, 16 * (n + 1))
                    for j in range(TPB):
                        last = nc.vector.bn_stats(stats[:, j, :], x_sb[:, j, :])
                    link(last, 1)
                    dve.sem_inc(apart, 1)
                    for j in range(TPB):
                        last = nc.vector.bn_aggr(mv[:, j, :], stats[:, j, :])
                    link(last, 2)
                    nc.vector.tensor_scalar(var_eps[:], mv[:, :, 1], 1e-5, None, ALU.add).then_inc(var_done, 1)
                if k == 1:
                    dve.wait_ge(rstd_done, n + 1)
                    need(dve, xt_ready, n)
                    for j in range(TPB):
                        last = nc.vector.tensor_scalar(xn[:, j, :], x_sb[:, j, :], mv[:, j, 0:1], rstd[:, j:j + 1],
                                                       ALU.subtract, ALU.mult)
                    last.then_inc(xn_done, 1)
                if k == 3:
                    dve.wait_ge(xhi_done, n + 1)
                    nc.vector.scalar_tensor_tensor(tokens_of(m.xlo, n), xt_ps[:].rearrange("p (s t) -> p s t", t=SS),
                                                   XSCALE, tokens_of(m.xhi, n), ALU.mult,
                                                   ALU.subtract).then_inc(xlo_done, 1)
                if k == 3 or k == 4:
                    h = k - 3
                    dve.wait_ge(logits_ready, 2 * n + h + 1)
                    nc.vector.tensor_tensor(logits[:, 2 * h:2 * h + 2, :], logit_ps[h], bias[:],
                                            ALU.add).then_inc(logits_done, 1)
                if k == 6:
                    dve.wait_ge(probs_done, n + 1)
                    dve.sem_inc(apart, 1)
                    for j in range(TPB):
                        last = nc.vector.max(top8[:, j, :], probs[:, j, :])
                    link(last, 3)
                    dve.sem_inc(apart, 1)
                    for j in range(TPB):
                        nc.vector.match_replace(rest[:, j, :], top8[:, j, :], probs[:, j, :], 0.0)
                    nc.vector.tensor_reduce(wsum[:], top8[:], AX.X, ALU.add).then_inc(step, 1)
                if k == 7:
                    dve.wait_ge(step, LINKS * n + 4)
                    link(nc.vector.tensor_scalar(wsum[:], wsum[:], 1e-9, None, ALU.add), 5)
                    link(nc.vector.reciprocal(wnorm[:], wsum[:]), 6)
                    nc.vector.tensor_tensor(picked[:], probs[:], rest[:], ALU.subtract)
                    link(nc.vector.tensor_scalar(wnorm[:], wnorm[:], m.kappa[:, 0:1], 2.5, ALU.mult, ALU.mult), 7)
                    for j in range(TPB):
                        last = nc.vector.tensor_scalar(comb[:, j, :], picked[:, j, :], wnorm[:, j:j + 1], None,
                                                       ALU.mult)
                    link(last, 8)
                    dve.sem_inc(comb_done, 1)
                if k == 8:
                    dve.wait_ge(comb_hi_done, n + 1)
                    nc.vector.tensor_tensor(parts[:, :, :, 1, :], comb[:].rearrange("p j (q e) -> p j q e", q=NQ),
                                            parts[:, :, :, 0, :], ALU.subtract).then_inc(parts_done, 1)
                if k == 9:
                    dve.wait_ge(comb_t_ready, 2 * n + 2)
                    nc.vector.tensor_copy(comb_t[:, half, 2:4, :], comb_ps[1]).then_inc(comb_b_done, 1)

            def weigh(b, bp, it, q, early):
                K = UNITS * b + 1 + NQ * it + q
                dve.wait_ge(silu_done, K + 1)
                dve.wait_ge(spread_done, (UNITS - 1) * b + NQ * it + q + 1)
                if not early:
                    dve.wait_ge(lo_done, K - 1)
                k = parity(bp, q)
                nc.vector.tensor_tensor(prod[k][:], act_out[k][:], spread_ps[q % 2][:],
                                        ALU.mult).then_inc(prod_done, 1)

            def copy_back(n):
                dve.wait_ge(back_ready, n + 2)
                nc.vector.tensor_copy(m.gate[:, ds(TPB * n, TPB), :], back_ps).then_inc(back_copied, 1)

            def body(b, bp, first):
                K = UNITS * b
                dve.wait_ge(silu_done, K + 1)
                if not first:
                    dve.wait_ge(lo_done, K - 1)
                nc.vector.tensor_scalar(prod[bp][0:INTER], act_out[bp][0:INTER], m.kappa[0:INTER, 0:1], None,
                                        ALU.mult).then_inc(prod_done, 1)
                weigh(b, bp, 0, 0, first)
                for q in range(1, NQ):
                    weigh(b, bp, 0, q, False)

                def turn(it):
                    for q in range(NQ):
                        weigh(b, bp, it, q, False)

                units_with_slots(dve, turn, slots_of(prepare, b, bp))
                if not first:
                    copy_back(b - 1)

            nc.vector.memset(w_dt[:], 0.0).then_inc(w_dt_zero, 1)
            dve.sem_inc(back_copied, 1)
            dve.wait_ge(params, NPARAM)
            for k in range(SLOTS):
                prepare(0, 0, k)
            blocks(dve, body)
            copy_back(NBLK - 1)


def prepare_decays(nc, m):
    with ExitStack() as ctx:
        def sem(name):
            return ctx.enter_context(nc.semaphore(name))

        def sb(name, shape, dt=F32):
            return ctx.enter_context(nc.sbuf_tensor("dec_" + name, shape, dt))

        R, HB, CPB = 2 * NH * NBLK, NH * NBLK, TPB
        bias_r, a_log, a_neg = (sb(n, [R, 1]) for n in ("dt_bias_rows", "a_log_rows", "a_neg"))
        rows = [m.experts[0:R, BLK * k:BLK * (k + 1)] for k in range(12)]
        raw, u, e, q, l2, dt, decay, inner, first, prefix = rows[0:10]
        part = [t[:, 0:BLK] for t in (rows[10].bitcast(BF16), rows[11].bitcast(BF16))]
        part.append(rows[10].bitcast(BF16)[:, BLK:])
        tot = sb("tot", [R, CPB])
        spread = sb("tot_spread", [R, R, CPB])
        ones = sb("ones", [R, P])
        carries = sb("carries", [R, CPB])
        w_stage = sb("w_stage", [P, 2, 3 * DI])
        w_max, w_all, w_pow2, w_up = (sb(n, [P, 2]) for n in ("w_max", "w_all", "w_pow2", "w_up"))
        back = sb("w_back", [P, 2])
        cw, skip, norm = sb("cw", [P, 2, 4, NCONV]), sb("skip", [P, 2, 2]), sb("norm", [P, 2, 2])
        wo_stage = sb("wo_stage", [P, 2, 2, DM])
        warm = sb("warm", [P, 1])
        tot_ps = ctx.enter_context(nc.psum_tensor("tot_ps", [P, R, CPB], F32))
        dt_ps = ctx.enter_context(nc.psum_tensor("dt_tok_ps", [P, CPB, R], F32))
        pre_ps = ctx.enter_context(nc.psum_tensor("pre_tok_ps", [P, CPB, R], F32))

        loaded, w_loaded, small = sem("rows_loaded"), sem("w_loaded"), sem("small_loaded")
        step, v_done, e_done, dt_done, decay_done = (sem(n) for n in (
            "vector_step", "softplus_in", "exp_done", "dt_done", "decay_done"))
        a_done, prefix_done, spread_done = sem("a_done"), sem("prefix_done"), sem("spread_done")
        parts_done, parts_stored, parts_loaded, tables_ready = (sem(n) for n in (
            "parts_done", "parts_stored", "parts_loaded", "tables_ready"))
        maxed, reduced, up_done, high_done = sem("w_maxed"), sem("w_reduced"), sem("w_up_done"), sem("w_high_done")
        pool_step = sem("pool_step")
        block = ctx.enter_context(nc.Block())

        @block.sync
        def _(sp):
            dt_rows = m.dram.dt_scratch.rearrange("n r t -> r n t")
            for d in range(2):
                for h in range(NH):
                    r = HB * d + NBLK * h
                    sp.dma_start(raw[r:r + NBLK, :], dt_rows[32 * d + h]).then_inc(loaded, 16)
            sp.dma_start(bias_r[:], m.dram.dt_bias).then_inc(loaded, 16)
            sp.dma_start(a_log[:], m.dram.a_log).then_inc(loaded, 16)
            sp.dma_start(carries[:], m.dram.carries).then_inc(loaded, 16)
            for d in range(2):
                sp.dma_start(w_stage[:, d, :], m.dram.w_in[d][:, 0:3 * DI]).then_inc(w_loaded, 16)
            for t, src in ((cw, m.dram.conv_w), (m.conv_b, m.dram.conv_b), (skip, m.dram.skip),
                           (norm, m.dram.norm_w), (wo_stage, m.dram.w_out)):
                sp.dma_start(t[:], src).then_inc(small, 16)
            sp.wait_ge(parts_done, 3)
            for k in range(3):
                sp.dma_start(m.dram.decay_scratch[k], part[k]).then_inc(parts_stored, 16)
            sp.wait_ge(parts_stored, 16 * 3)
            for k in range(3):
                for d in range(2):
                    r = 3 * NH * d + NH * k
                    sp.dma_start(m.decay_parts[r:r + NH, :],
                                 m.dram.decay_scratch[k, HB * d:HB * (d + 1), :]
                                 .rearrange("(h b) t -> h (b t)", h=NH)).then_inc(parts_loaded, 16)
            sp.wait_ge(parts_loaded, 16 * 6)

        @block.vector
        def _(dve):
            n = [0]

            def link(ins):
                n[0] += 1
                ins.then_inc(step, 1)
                dve.wait_ge(step, n[0])

            V = nc.vector
            V.memset(ones[:], 1.0)
            V.memset(m.state[:], 0.0)
            dve.wait_ge(loaded, 16 * 11)
            link(V.tensor_scalar(raw[:], raw[:], bias_r[:, 0:1], None, ALU.add))
            link(V.tensor_scalar(u[:], raw[:], -1.0, None, ALU.mult))
            V.tensor_tensor(u[:], u[:], raw[:], ALU.min).then_inc(v_done, 1)
            dve.wait_ge(e_done, 1)
            link(V.tensor_scalar(u[:], e[:], 2.0, None, ALU.add))
            link(V.reciprocal(u[:], u[:]))
            link(V.tensor_tensor(u[:], e[:], u[:], ALU.mult))
            link(V.tensor_tensor(l2[:], u[:], u[:], ALU.mult))
            link(V.tensor_scalar(q[:], l2[:], 1.0 / 19, None, ALU.mult))
            for k in range(8, 0, -1):
                link(V.scalar_tensor_tensor(q[:], q[:], 1.0 / (2 * k + 1), l2[:], ALU.add, ALU.mult))
            link(V.scalar_tensor_tensor(q[:], q[:], 1.0, u[:], ALU.add, ALU.mult))
            link(V.tensor_scalar(raw[:], raw[:], 0.0, None, ALU.max))
            V.scalar_tensor_tensor(dt[:], q[:], 2.0, raw[:], ALU.mult, ALU.add).then_inc(dt_done, 1)
            dve.wait_ge(a_done, 1)
            V.tensor_scalar(a_neg[:], a_neg[:], -1.0, None, ALU.mult).then_inc(a_done, 1)
            dve.wait_ge(decay_done, 1)
            link(V.tensor_copy(inner[:], decay[:]))
            V.memset(inner[0:HB, 0::P], 0.0)
            link(V.memset(inner[HB:R, P - 1::P], 0.0))
            link(V.tensor_tensor(first[:], decay[:], inner[:], ALU.subtract))
            V.tensor_tensor_scan(prefix[0:HB, :], inner[0:HB, :], first[0:HB, :], 0.0, ALU.mult, ALU.add)
            link(V.tensor_tensor_scan(prefix[HB:R, ::-1], inner[HB:R, ::-1], first[HB:R, ::-1], 0.0,
                                      ALU.mult, ALU.add))
            V.tensor_copy(tot[0:HB, :], prefix[0:HB, P - 1::P])
            link(V.tensor_copy(tot[HB:R, :], prefix[HB:R, 0::P]))
            V.tensor_tensor(tot[:], tot[:], carries[:], ALU.mult)
            by_chunk = prefix.rearrange("r (c t) -> r c t", t=P)
            V.tensor_tensor(by_chunk, by_chunk, carries[:].unsqueeze(2).broadcast_to([R, CPB, P]),
                            ALU.mult).then_inc(prefix_done, 1)
            dve.wait_ge(prefix_done, 1)
            V.tensor_tensor(spread[:], m.ident[0:R, 0:R].unsqueeze(2).broadcast_to([R, R, CPB]),
                            tot[:].unsqueeze(1).broadcast_to([R, R, CPB]), ALU.mult).then_inc(spread_done, 1)
            link(V.tensor_copy(part[0][:], inner[:]))
            for k in (1, 2):
                link(V.tensor_tensor(inner[:], inner[:], part[k - 1][:], ALU.subtract))
                link(V.tensor_copy(part[k][:], inner[:]))
            dve.sem_inc(parts_done, 3)
            dve.wait_ge(w_loaded, 32)
            for d in range(2):
                last = V.tensor_reduce(w_max[:, d:d + 1], w_stage[:, d, :], AX.X, ALU.max,
                                       apply_absolute_value=True)
            link(last)
            V.tensor_scalar(w_max[:], w_max[:], 1e-30, None, ALU.max).then_inc(maxed, 1)
            dve.wait_ge(reduced, 1)
            link(V.tensor_scalar(w_pow2[:].bitcast(I32), w_all[:].bitcast(I32), 0x7F800000, None,
                                 ALU.bitwise_and))
            link(V.reciprocal(w_up[:], w_pow2[:]))
            V.tensor_scalar(w_up[:], w_up[:], WTOP, None, ALU.mult).then_inc(up_done, 1)
            link(V.tensor_scalar(m.in_back[:], w_pow2[:], 1.0 / (XSCALE * WTOP), None, ALU.mult))
            dve.wait_ge(small, 16 * 5)
            for d in range(2):
                V.tensor_scalar(m.conv_w[:, d], cw[:, d], m.in_back[:, d:d + 1], None, ALU.mult)
                for k in range(2):
                    V.tensor_scalar(m.skip_diag[:, d, k, :], m.ident[:], skip[:, d, k:k + 1], None, ALU.mult)
                    V.tensor_scalar(m.w_out[:, d, k, :], wo_stage[:, d, k, :], norm[:, d, k:k + 1], 0.5,
                                    ALU.mult, ALU.mult)
            for h in range(NH):
                V.tensor_copy(m.ident4[:, h, :], m.ident[:])
            for d in range(2):
                dve.wait_ge(high_done, d + 1)
                V.scalar_tensor_tensor(m.win_lo[:, d, :], w_stage[:, d, :], w_up[:, d:d + 1],
                                       m.win_hi[:, d, :], ALU.mult, ALU.subtract)
            dve.wait_ge(tables_ready, 3)
            for d in range(2):
                rows = slice(HB * d, HB * (d + 1))
                V.tensor_copy(m.tot[:, d].rearrange("p (b c) h -> p h b c", b=NBLK),
                              tot_ps[:, rows, :].rearrange("p (h b) c -> p h b c", h=NH))
                for t, src in ((m.dt_tok, dt_ps), (m.prefix_tok, pre_ps)):
                    V.tensor_copy(t[:, d].rearrange("p (b c) h -> p h b c", b=NBLK),
                                  src[:, :, rows].rearrange("p c (h b) -> p h b c", h=NH))

        @block.gpsimd
        def _(pool):
            nc.gpsimd.memset(m.head_select[:], 0.0).then_inc(pool_step, 1)
            pool.wait_ge(pool_step, 1)
            for k in range(3):
                nc.gpsimd.affine_select(out=m.head_select[:], in_=m.head_select[:], compare_op=ALU.not_equal,
                                        fill=1.0, base=-NH * k, pattern=[[-3 * NH, 2], [-1, NH], [0, P]],
                                        channel_multiplier=1).then_inc(pool_step, 1)
                pool.wait_ge(pool_step, k + 2)
            pool.wait_ge(maxed, 1)
            nc.gpsimd.partition_all_reduce(w_all[:], w_max[:], P, RMAX).then_inc(reduced, 1)

        @block.scalar
        def _(act):
            nc.scalar.activation(warm[:], m.minus_half[:, 0:1], ACT.Exp)
            act.wait_ge(loaded, 16 * 11)
            nc.scalar.activation(a_neg[:], a_log[:], ACT.Exp).then_inc(a_done, 1)
            act.wait_ge(v_done, 1)
            nc.scalar.activation(e[:], u[:], ACT.Exp).then_inc(e_done, 1)
            act.wait_ge(dt_done, 1)
            act.wait_ge(a_done, 2)
            nc.scalar.activation(decay[:], dt[:], ACT.Exp, scale=a_neg[:, 0:1]).then_inc(decay_done, 1)
            act.wait_ge(up_done, 1)
            for d in range(2):
                nc.scalar.activation(m.win_hi[:, d, :], w_stage[:, d, :], ACT.Copy,
                                     scale=w_up[:, d:d + 1]).then_inc(high_done, 1)

        @block.tensor
        def _(pe):
            pe.wait_ge(dt_done, 1)
            for c in range(CPB):
                last = nc.tensor.transpose(dt_ps[:, c, :], dt[:, c * P:(c + 1) * P], m.ident[0:R, 0:R])
            last.then_inc(tables_ready, 1)
            pe.wait_ge(prefix_done, 1)
            for c in range(CPB):
                last = nc.tensor.transpose(pre_ps[:, c, :], prefix[:, c * P:(c + 1) * P], m.ident[0:R, 0:R])
            last.then_inc(tables_ready, 1)
            pe.wait_ge(spread_done, 1)
            nc.tensor.matmul(tot_ps[:], ones[:], spread[:], start=True, stop=True).then_inc(tables_ready, 1)


def run_ssm(nc, m):
    with ExitStack() as ctx:
        def sem(name):
            return ctx.enter_context(nc.semaphore(name))

        def sb(name, shape, dt=F32):
            return ctx.enter_context(nc.sbuf_tensor("ssm_" + name, shape, dt))

        def ps(name, shape, dt=F32):
            return ctx.enter_context(nc.psum_tensor("ssm_" + name, shape, dt))

        TILE = 8
        UPS = 4
        X0, X1, B, C = range(4)
        conv_out = [[sb(f"conv_out{p}{d}", [P, 4, SS]) for d in range(2)] for p in range(2)]
        conv_acc = [sb(f"conv_acc{i}", [P, SS]) for i in range(2)]
        conv_tap1 = [sb(f"conv_tap1{i}", [P, SS]) for i in range(2)]
        reach = [sb(f"reach{d}", [P, NH, P]) for d in range(2)]
        score = [sb(f"score{d}", [P, NH, P]) for d in range(2)]
        x_dt = [sb(f"x_dt{d}", [P, NH, HD]) for d in range(2)]
        x_end = [sb(f"x_end{d}", [P, NH, HD]) for d in range(2)]
        b_tok = [sb(f"b_tok{d}", [P, DS]) for d in range(2)]
        z_act = [sb(f"z_act{d}", [P, DI]) for d in range(2)]
        carried = sb("carried", [P, NH, HD])
        y_sb = [sb(f"y_sb{d}", [P, DI]) for d in range(2)]
        gated_t = [sb(f"gated_t{d}", [P, 2, P]) for d in range(2)]
        squares = conv_tap1[0]
        mean_sq = [sb(f"mean_sq{d}", [P, 1]) for d in range(2)]
        mean_eps = [sb(f"mean_eps{d}", [P, 1]) for d in range(2)]
        rms = [sb(f"rms{d}", [P, 1]) for d in range(2)]
        warm = sb("warm", [P, 1])

        u_ps = [ps(f"u_ps{i}", [P, SS + NCONV - 1]) for i in range(2)]
        decay_ps = ps("decay_ps", [P, NH, P])
        gx_ps = ps("gx_ps", [P, 3, P])
        bz_ps = ps("bz_ps", [P, 3, P])
        y_ps = ps("y_ps", [P, 2, DI])
        s_ps = ps("s_ps", [P, NH, HD])
        o_ps = ps("o_ps", [P, 3, P])

        names = ("u_ready two_taps_ready two_taps_added taps_done taps_step xs_done gx_ready decay_ready bz_ready scan_done "
                 "xdt_done xend_done z_done y_ready s_ready carried_done yprev_done y_done "
                 "state_done gated_done square_done eps_done rms_done gt_ready gt_copied out_ready out_done")
        S = {n: sem(n) for n in names.split()}
        block = ctx.enter_context(nc.Block())

        def supersteps(eng, prologue, slot, epilogue):
            prologue()

            def step(f, par):
                s = (f, NSS - 1 - f) if isinstance(f, int) else (f, eng.snap(f * (-1) + (NSS - 1)))
                last = isinstance(f, int) and f == NSS - 1
                for j in range(UPS):
                    slot(s, par, j, last)

            step(0, 0)
            step(1, 1)
            with eng.Fori(1, NSS // 2 - 1) as i:
                for par in range(2):
                    step(2 * i + par, par)
            step(NSS - 2, 0)
            step(NSS - 1, 1)
            epilogue()

        FIRST, LAST = (0, NSS - 1), (NSS - 1, 0)

        def after(s):
            return s[0] + 1, s[1] - 1

        def before(s):
            return s[0] - 1, s[1] + 1

        def chunk_in(j):
            d, c = j % 2, j // 2
            return c if d == 0 else 1 - c

        def chunk_of(eng, s, j):
            chunk = 2 * s[j % 2] + chunk_in(j)
            return chunk if isinstance(chunk, int) else eng.snap(chunk)

        def unit_before(s, par, j, back):
            if j >= back:
                return s, par, j - back
            return before(s), 1 - par, j - back + UPS

        def is_unit(s, j, back):
            return not isinstance(s[0], int) or UPS * s[0] + j >= back

        def next_unit(s, par, j):
            return (s, par, j + 1) if j + 1 < UPS else (after(s), 1 - par, 0)

        def tokens(t, s, d, first, count):
            return t[:, ds(s[d], 1), first:first + count].rearrange("p o t -> p (o t)")

        @block.tensor
        def _(pe):
            MM = nc.tensor.matmul

            def conv_tile(s, i):
                T, d, g = TILE * s[0] + i, i // 4, i % 4
                need(pe, S["taps_done"], T - 1)
                first = HALO - (NCONV - 1) if d == 0 else HALO
                cols = slice(DI + g * P, DI + (g + 1) * P)
                xh, xl = (tokens(t, s, d, first, SS + NCONV - 1) for t in (m.xhi, m.xlo))
                MM(u_ps[i % 2][:], m.win_hi[:, d, cols], xh, start=True, stop=False)
                MM(u_ps[i % 2][:], m.win_hi[:, d, cols], xl, start=False, stop=False)
                MM(u_ps[i % 2][:], m.win_lo[:, d, cols], xh, start=False, stop=True).then_inc(S["u_ready"], 1)

            def decays(s, j):
                K, d = UPS * s[0] + j, j % 2
                chunk = chunk_of(pe, s, j)
                need(pe, S["scan_done"], K)
                for h in range(NH):
                    last = MM(decay_ps[:, h, :], m.head_select[:, d, h, :], m.decay_parts[:, ds(chunk * P, P)],
                              start=True, stop=True)
                last.then_inc(S["decay_ready"], 1)

            def front(s, par, j):
                K, d, c = UPS * s[0] + j, j % 2, chunk_in(j)
                xs, at = conv_out[par][d], slice(c * P, (c + 1) * P)
                need(pe, S["xs_done"], TILE * s[0] + 4 * (d + 1))
                need(pe, S["xdt_done"], K)
                MM(gx_ps[:, 0, :], xs[:, B, at], xs[:, C, at], start=True, stop=True)
                nc.tensor.transpose(gx_ps[:, 1, :], xs[:, X0, at], m.ident[:])
                nc.tensor.transpose(gx_ps[:, 2, :], xs[:, X1, at], m.ident[:]).then_inc(S["gx_ready"], 1)
                need(pe, S["z_done"], K)
                nc.tensor.transpose(bz_ps[:, 0, :], xs[:, B, at], m.ident[:])
                zh, zl = (tokens(t, s, d, HALO + c * P, P) for t in (m.xhi, m.xlo))
                z = bz_ps[:, 1:3, :].rearrange("p a b -> p (a b)")
                MM(z, zh, m.win_hi[:, d, 0:DI], start=True, stop=False)
                MM(z, zh, m.win_lo[:, d, 0:DI], start=False, stop=False)
                MM(z, zl, m.win_hi[:, d, 0:DI], start=False, stop=True).then_inc(S["bz_ready"], 1)

            def middle(s, par, j):
                K, d, c = UPS * s[0] + j, j % 2, chunk_in(j)
                xs, at = conv_out[par][d], slice(c * P, (c + 1) * P)
                need(pe, S["y_done"], K)
                for k in range(2):
                    MM(y_ps[:, 0, k * P:(k + 1) * P], xs[:, k, at], m.skip_diag[:, d, k, :],
                       start=(k == 0), stop=False, skip_group_check=True)
                need(pe, S["state_done"], K - 1)
                MM(y_ps[:, 1, :], xs[:, C, at], m.state[:, d, :], start=False, stop=False,
                   skip_group_check=True)
                need(pe, S["xdt_done"], K + 1)
                for h in range(NH):
                    last = MM(y_ps[:, 0, h * HD:(h + 1) * HD], score[d][:, h, :], x_dt[d][:, h, :],
                              start=False, stop=(h == NH - 1), skip_group_check=True)
                last.then_inc(S["y_ready"], 1)
                need(pe, S["xend_done"], K + 1)
                need(pe, S["z_done"], K + 1)
                need(pe, S["state_done"], K)
                MM(s_ps[:], b_tok[d][:], x_end[d][:], start=True, stop=True).then_inc(S["s_ready"], 1)

            def back_a(s, j):
                K, d = UPS * s[0] + j, j % 2
                need(pe, S["gated_done"], K + 1)
                need(pe, S["out_done"], K)
                for k in range(2):
                    last = nc.tensor.transpose(o_ps[:, k, :], y_sb[d][:, k * P:(k + 1) * P], m.ident[:])
                last.then_inc(S["gt_ready"], 1)

            def back_b(s, j):
                K, d = UPS * s[0] + j, j % 2
                need(pe, S["gt_copied"], K + 1)
                for k in range(2):
                    last = MM(o_ps[:, 2, :], gated_t[d][:, k, :], m.w_out[:, d, k, :],
                              start=(k == 0), stop=(k == 1))
                last.then_inc(S["out_ready"], 1)

            def prologue():
                for i in range(TILE):
                    conv_tile(FIRST, i)
                decays(FIRST, 0)
                front(FIRST, 0, 0)

            def slot(s, par, j, last):
                if not (last and j == UPS - 1):
                    sn, _, jn = next_unit(s, par, j)
                    decays(sn, jn)
                if not last:
                    conv_tile(after(s), 2 * j)
                    conv_tile(after(s), 2 * j + 1)
                if not (last and j == UPS - 1):
                    front(*next_unit(s, par, j))
                if is_unit(s, j, 2):
                    s2, _, j2 = unit_before(s, par, j, 2)
                    back_b(s2, j2)
                middle(s, par, j)
                if is_unit(s, j, 1):
                    s1, _, j1 = unit_before(s, par, j, 1)
                    back_a(s1, j1)

            def epilogue():
                back_b(LAST, UPS - 2)
                back_a(LAST, UPS - 1)
                back_b(LAST, UPS - 1)

            supersteps(pe, prologue, slot, epilogue)

        @block.scalar
        def _(act):
            def two_taps(s, i):
                T, d, g = TILE * s[0] + i, i // 4, i % 4
                need(act, S["u_ready"], T + 1)
                need(act, S["xs_done"], T - 1)
                at = 0 if d == 0 else NCONV - 1
                need(act, S["square_done"], UPS * (s[0] - 1) + i // 2 - 1)
                nc.scalar.activation(conv_acc[i % 2][:], u_ps[i % 2][:, at:at + SS], ACT.Identity,
                                     bias=m.conv_b[:, d, g:g + 1],
                                     scale=m.conv_w[:, d, g, 0:1])
                at = 1 if d == 0 else NCONV - 2
                nc.scalar.activation(conv_tap1[i % 2][:], u_ps[i % 2][:, at:at + SS], ACT.Copy,
                                     scale=m.conv_w[:, d, g, 1:2]).then_inc(S["two_taps_ready"], 1)

            def conv_silu(s, par, i):
                T, d, g = TILE * s[0] + i, i // 4, i % 4
                need(act, S["taps_done"], T + 1)
                need(act, S["s_ready"], UPS * (s[0] - 1))
                nc.scalar.activation(conv_out[par][d][:, g, :], conv_acc[i % 2][:],
                                     ACT.Silu).then_inc(S["xs_done"], 1)

            def front(s, j):
                K, d = UPS * s[0] + j, j % 2
                need(act, S["bz_ready"], K + 1)
                need(act, S["s_ready"], K - 1)
                nc.scalar.activation(b_tok[d][:], bz_ps[:, 0, :], ACT.Copy)
                need(act, S["gated_done"], K - 1)
                nc.scalar.activation(z_act[d][:], bz_ps[:, 1:3, :].rearrange("p a b -> p (a b)"), ACT.Silu,
                                     scale=m.in_back[:, d:d + 1]).then_inc(S["z_done"], 1)

            def square(s, j):
                K, d = UPS * s[0] + j, j % 2
                need(act, S["gated_done"], K + 1)
                tiles = 2 * K + TILE + 3
                need(act, S["two_taps_added"], min(tiles, TILE * NSS) if isinstance(K, int) else tiles)
                need(act, S["eps_done"], K - 1)
                nc.scalar.activation(squares[:], y_sb[d][:], ACT.Square, scale=DI ** -0.5,
                                     accum_out=mean_sq[d][:]).then_inc(S["square_done"], 1)

            def copy_t(s, j):
                K, d = UPS * s[0] + j, j % 2
                need(act, S["gt_ready"], K + 1)
                need(act, S["out_ready"], K - 1)
                nc.scalar.activation(gated_t[d][:], o_ps[:, 0:2, :], ACT.Copy).then_inc(S["gt_copied"], 1)

            def out(s, j):
                K, d, chunk = UPS * s[0] + j, j % 2, chunk_of(act, s, j)
                need(act, S["out_ready"], K + 1)
                need(act, S["rms_done"], K + 1)
                nc.scalar.activation(m.out[:, d, ds(chunk, 1), :].rearrange("p o d -> p (o d)"),
                                     o_ps[:, 2, :], ACT.Copy, scale=rms[d][:, 0:1]).then_inc(S["out_done"], 1)

            def prologue():
                nc.scalar.activation(warm[:], m.minus_half[:, 0:1], ACT.Silu)
                for i in range(0, TILE, 2):
                    for k in (i, i + 1):
                        two_taps(FIRST, k)
                    for k in (i, i + 1):
                        conv_silu(FIRST, 0, k)
                front(FIRST, 0)

            def slot(s, par, j, last):
                if not last:
                    two_taps(after(s), 2 * j)
                    two_taps(after(s), 2 * j + 1)
                if not (last and j == UPS - 1):
                    sn, _, jn = next_unit(s, par, j)
                    front(sn, jn)
                if is_unit(s, j, 1):
                    s1, _, j1 = unit_before(s, par, j, 1)
                    square(s1, j1)
                if is_unit(s, j, 2):
                    s2, _, j2 = unit_before(s, par, j, 2)
                    out(s2, j2)
                if not last:
                    conv_silu(after(s), 1 - par, 2 * j)
                    conv_silu(after(s), 1 - par, 2 * j + 1)
                if is_unit(s, j, 1):
                    s1, _, j1 = unit_before(s, par, j, 1)
                    copy_t(s1, j1)

            def epilogue():
                out(LAST, UPS - 2)
                square(LAST, UPS - 1)
                copy_t(LAST, UPS - 1)
                out(LAST, UPS - 1)

            supersteps(act, prologue, slot, epilogue)

        @block.vector
        def _(dve):
            V = nc.vector

            def taps(s, i0):
                for tap in range(2, NCONV):
                    for i in (i0, i0 + 1):
                        T, d, g = TILE * s[0] + i, i // 4, i % 4
                        need(dve, S["two_taps_added" if tap == 2 else "taps_step"], T + 1)
                        at = tap if d == 0 else NCONV - 1 - tap
                        V.scalar_tensor_tensor(conv_acc[i % 2][:], u_ps[i % 2][:, at:at + SS],
                                               m.conv_w[:, d, g, tap:tap + 1], conv_acc[i % 2][:],
                                               ALU.mult, ALU.add
                                               ).then_inc(S["taps_done" if tap == NCONV - 1 else "taps_step"], 1)

            def front(s, j):
                K, d, chunk = UPS * s[0] + j, j % 2, chunk_of(dve, s, j)
                flat = [t[:].rearrange("p h t -> p (h t)") for t in (reach[d], decay_ps, m.ident4)]
                if d == 1:
                    flat = [t[:, ::-1] for t in flat]
                need(dve, S["decay_ready"], K + 1)
                need(dve, S["xend_done"], K - 1)
                V.tensor_tensor_scan(flat[0], flat[1], flat[2], 0.0, ALU.mult,
                                     ALU.add).then_inc(S["scan_done"], 1)
                need(dve, S["gx_ready"], K + 1)
                need(dve, S["s_ready"], K - 1)
                V.tensor_tensor(x_dt[d][:], gx_ps[:, 1:3, :].rearrange("p a (h c) -> p (a h) c", c=HD),
                                m.dt_tok[:, d, ds(chunk, 1), :].rearrange("p o h -> p (o h)").unsqueeze(2)
                                .broadcast_to([P, NH, HD]), ALU.mult)
                need(dve, S["scan_done"], K + 1)
                V.tensor_tensor(score[d][:], reach[d][:], gx_ps[:, 0:1, :].broadcast_to([P, NH, P]),
                                ALU.mult).then_inc(S["xdt_done"], 1)

            def middle(s, j):
                K, d, chunk = UPS * s[0] + j, j % 2, chunk_of(dve, s, j)
                need(dve, S["y_ready"], K + 1)
                need(dve, S["gt_ready"], K - 1)
                need(dve, S["square_done"], K - 1)
                V.tensor_tensor(y_sb[d][:].rearrange("p (h c) -> p h c", c=HD), y_ps[:, 1, :].rearrange("p (h c) -> p h c", c=HD),
                                m.prefix_tok[:, d, ds(chunk, 1), :].rearrange("p o h -> p (o h)").unsqueeze(2)
                                .broadcast_to([P, NH, HD]), ALU.mult).then_inc(S["yprev_done"], 1)
                need(dve, S["yprev_done"], K + 1)
                V.tensor_tensor(y_sb[d][:], y_ps[:, 0, :], y_sb[d][:], ALU.add).then_inc(S["y_done"], 1)
                need(dve, S["s_ready"], K + 1)
                need(dve, S["carried_done"], K + 1)
                V.tensor_tensor(m.state[:, d, :], s_ps[:].rearrange("p h c -> p (h c)"),
                                carried[:].rearrange("p h c -> p (h c)"), ALU.add
                                ).then_inc(S["state_done"], 1)

            def prologue():
                for i in range(0, TILE, 2):
                    taps(FIRST, i)
                front(FIRST, 0)

            def slot(s, par, j, last):
                if not (last and j == UPS - 1):
                    sn, _, jn = next_unit(s, par, j)
                    front(sn, jn)
                if not last:
                    taps(after(s), 2 * j)
                middle(s, j)

            supersteps(dve, prologue, slot, lambda: None)

        @block.gpsimd
        def _(pool):
            G = nc.gpsimd

            def add_taps(s, i):
                need(pool, S["two_taps_ready"], TILE * s[0] + i + 1)
                G.tensor_tensor(conv_acc[i % 2][:], conv_acc[i % 2][:], conv_tap1[i % 2][:],
                                ALU.add).then_inc(S["two_taps_added"], 1)

            def front(s, j):
                K, d = UPS * s[0] + j, j % 2
                end = P - 1 if d == 0 else 0
                need(pool, S["xdt_done"], K + 1)
                need(pool, S["s_ready"], K - 1)
                G.tensor_tensor(x_end[d][:], x_dt[d][:], reach[d][:, :, end:end + 1].broadcast_to([P, NH, HD]),
                                ALU.mult).then_inc(S["xend_done"], 1)

            def middle(s, j):
                K, d, chunk = UPS * s[0] + j, j % 2, chunk_of(pool, s, j)
                need(pool, S["state_done"], K)
                G.tensor_tensor(carried[:], m.state[:, d, :].rearrange("p (h c) -> p h c", c=HD),
                                m.tot[:, d, ds(chunk, 1), :].rearrange("p o h -> p (o h)").unsqueeze(2)
                                .broadcast_to([P, NH, HD]), ALU.mult).then_inc(S["carried_done"], 1)
                need(pool, S["y_done"], K + 1)
                need(pool, S["z_done"], K + 1)
                G.tensor_tensor(y_sb[d][:], y_sb[d][:], z_act[d][:], ALU.mult).then_inc(S["gated_done"], 1)

            def norm(s, j):
                K, d = UPS * s[0] + j, j % 2
                need(pool, S["square_done"], K + 1)
                need(pool, S["rms_done"], K - 1)
                G.tensor_tensor(mean_eps[d][:], mean_sq[d][:], m.eps[:], ALU.add).then_inc(S["eps_done"], 1)
                need(pool, S["eps_done"], K + 1)
                need(pool, S["out_done"], K - 1)
                G.tensor_tensor(rms[d][:], mean_eps[d][:], m.minus_half[:, 0:1],
                                ALU.pow).then_inc(S["rms_done"], 1)

            def prologue():
                for i in range(TILE):
                    add_taps(FIRST, i)
                front(FIRST, 0)

            def slot(s, par, j, last):
                if not last:
                    add_taps(after(s), 2 * j)
                    add_taps(after(s), 2 * j + 1)
                if is_unit(s, j, 2):
                    s2, _, j2 = unit_before(s, par, j, 2)
                    norm(s2, j2)
                if not (last and j == UPS - 1):
                    sn, _, jn = next_unit(s, par, j)
                    front(sn, jn)
                middle(s, j)

            def epilogue():
                norm(LAST, UPS - 2)
                norm(LAST, UPS - 1)

            supersteps(pool, prologue, slot, epilogue)


def write_out(nc, m):
    with ExitStack() as ctx:
        TPG = 8
        NG = TILES // TPG
        x_sb = [ctx.enter_context(nc.sbuf_tensor(f"x_res{k}", [P, TPG, DM], F32)) for k in range(2)]
        both = [ctx.enter_context(nc.sbuf_tensor(f"both{k}", [P, TPG, DM], F32)) for k in range(2)]
        res = [ctx.enter_context(nc.sbuf_tensor(f"res{k}", [P, TPG, DM], F32)) for k in range(2)]
        loaded = [ctx.enter_context(nc.semaphore(f"x_loaded{k}")) for k in range(2)]
        summed = ctx.enter_context(nc.semaphore("summed"))
        scaled = ctx.enter_context(nc.semaphore("scaled"))
        added = ctx.enter_context(nc.semaphore("added"))
        stored = [ctx.enter_context(nc.semaphore(f"stored{k}")) for k in range(2)]
        block = ctx.enter_context(nc.Block())

        def tiles(t, g):
            return t[:, TPG * g:TPG * (g + 1), :]

        @block.sync
        def _(sp):
            for g in range(NG):
                if g >= 2:
                    sp.wait_ge(added, g - 1)
                sp.dma_start(x_sb[g % 2][:], m.dram.x_tiles[:, TPG * g:TPG * (g + 1), :]
                             ).then_inc(loaded[g % 2], 16)

        @block.vector
        def _(dve):
            for g in range(NG):
                if g >= 2:
                    dve.wait_ge(added, g - 1)
                nc.vector.tensor_tensor(both[g % 2][:], tiles(m.out[:, 0], g), tiles(m.out[:, 1], g),
                                        ALU.add).then_inc(summed, 1)
                dve.wait_ge(summed, g + 1)
                nc.vector.tensor_tensor(both[g % 2][:], both[g % 2][:], tiles(m.gate, g),
                                        ALU.mult).then_inc(scaled, 1)

        @block.gpsimd
        def _(pool):
            for g in range(NG):
                pool.wait_ge(scaled, g + 1)
                pool.wait_ge(loaded[g % 2], 16 * (g // 2 + 1))
                if g >= 2:
                    pool.wait_ge(stored[g % 2], 16 * (g // 2))
                nc.gpsimd.tensor_tensor(res[g % 2][:], both[g % 2][:], x_sb[g % 2][:], ALU.add).then_inc(added, 1)

        @block.scalar
        def _(act):
            for g in range(NG):
                act.wait_ge(added, g + 1)
                act.dma_start(m.dram.out_tiles[:, TPG * g:TPG * (g + 1), :], res[g % 2][:]
                              ).then_inc(stored[g % 2], 16)
            for k in range(2):
                act.wait_ge(stored[k], 16 * (NG // 2))


def build(nc, ins, outs):
    m, d = Memory(), Memory()
    m.dram = d
    d.x_blocks = ins["x"].rearrange("b t d -> (b t) d").rearrange("(n j p) d -> n p j d", p=P, j=TPB)
    d.w_gate, d.w_down = ins["w_gate"], ins["w_down"]
    d.w_gate_shared, d.w_down_shared = ins["w_gate_shared"], ins["w_down_shared"]
    d.router = ins["router"]
    d.expert_bias = ins["expert_bias"].rearrange("(o e) -> o e", o=1).to_broadcast([P, NE])
    d.w_in = [ins["w_in_f"], ins["w_in_b"]]
    d.carries = ins["carries"]
    d.dt_bias, d.a_log, d.conv_w, d.conv_b = ins["dt_bias"], ins["a_log"], ins["conv_w"], ins["conv_b"]
    d.skip, d.norm_w, d.w_out = ins["skip"], ins["norm_w"], ins["w_out"]
    flat = "b t d -> (b t) d"
    d.x_tiles = ins["x"].rearrange(flat).rearrange("(n p) d -> p n d", p=P)
    d.out_tiles = outs["out"].rearrange(flat).rearrange("(n p) d -> p n d", p=P)
    d.dt_scratch = nc.dram_tensor("dt_scratch", [NBLK, 36, BLK], F32, kind="Internal").ap()
    d.decay_scratch = nc.dram_tensor("decay_scratch", [3, 2 * NH * NBLK, BLK], BF16, kind="Internal").ap()
    with ExitStack() as ctx:
        def sb(name, shape, dt=F32):
            return ctx.enter_context(nc.sbuf_tensor(name, shape, dt))

        m.experts = sb("experts", [P, 2 * NE * INTER])
        w16 = m.experts[:].bitcast(F16).rearrange("p (k n) -> p k n", k=4)
        m.wg_hi, m.wg_lo, m.wd_hi, m.wd_lo = (w16[:, k, :] for k in range(4))
        m.gate = sb("gate", [P, TILES, DM])
        m.xhi, m.xlo = sb("xhi", [P, NSS, SW], F16), sb("xlo", [P, NSS, SW], F16)
        m.gate_back, m.moe_back, m.kappa = sb("gate_back", [P, 1]), sb("moe_back", [P, 1]), sb("kappa", [P, 1])
        m.ident, m.minus_half, m.eps = sb("ident", [P, P]), sb("minus_half", [P, TPB]), sb("eps", [P, 1])
        with (nc.sbuf_tensor("sh_hi", [P, 2, P], F16) as m.sh_hi, nc.sbuf_tensor("sh_lo", [P, 2, P], F16) as m.sh_lo,
              nc.sbuf_tensor("pair_select", [2 * EQ, EQ * INTER], F16) as m.pair_select,
              nc.sbuf_tensor("ident16", [P, P], F16) as m.ident16):
            scale_weights(nc, m)
            run_experts(nc, m)
        m.out = m.experts[:, 0:2 * TILES * DM].rearrange("p (d n c) -> p d n c", d=2, n=TILES)
        m.decay_parts = m.experts[0:6 * NH, 2 * TILES * DM:].bitcast(BF16)
        m.state = sb("state", [P, 2, DI])
        m.win_hi, m.win_lo = sb("win_hi", [P, 2, 3 * DI], F16), sb("win_lo", [P, 2, 3 * DI], F16)
        m.in_back = sb("in_back", [P, 2])
        m.conv_w, m.conv_b = sb("conv_w", [P, 2, 4, NCONV]), sb("conv_b", [P, 2, 4])
        m.skip_diag = sb("skip_diag", [P, 2, 2, P])
        m.w_out = sb("w_out", [P, 2, 2, DM])
        m.ident4 = sb("ident4", [P, NH, P], BF16)
        m.head_select = sb("head_select", [6 * NH, 2, NH, P], BF16)
        m.tot, m.dt_tok, m.prefix_tok = (sb(n, [P, 2, TILES, NH]) for n in ("tot_all", "dt_tok", "prefix_tok"))
        prepare_decays(nc, m)
        run_ssm(nc, m)
        write_out(nc, m)


def kernel_inputs(inputs):
    g = {k: np.asarray(v) for k, v in inputs.items()}
    c = np.ascontiguousarray
    a = {"x": g["L0_attn_u"], "expert_bias": g["L0_ffn_expert_bias"]}
    a["w_gate"] = c(g["L0_ffn_w_gate"].reshape(NE * INTER, DM).T)
    a["w_down"] = c(g["L0_ffn_w_down"].transpose(0, 2, 1).reshape(NE // 2, P, DM).transpose(1, 0, 2)
                    .reshape(P, NE * INTER))
    a["w_gate_shared"] = c(g["L0_ffn_w_gate_shared"].T)
    a["w_down_shared"] = c(g["L0_ffn_w_down_shared"].T)
    a["router"] = c(g["L0_ffn_router_w"].T)
    both = {k: [g[f"L0_attn_{k}_{s}"] for s in "fb"]
            for k in ("Wi", "conv_w", "conv_b", "dt_bias", "A_log", "D", "norm_w", "Wo")}
    a["w_in_f"], a["w_in_b"] = (c(w.T) for w in both["Wi"])
    a["dt_bias"] = np.repeat(np.concatenate(both["dt_bias"]), NBLK).reshape(-1, 1)
    a["a_log"] = np.repeat(np.concatenate(both["A_log"]), NBLK).reshape(-1, 1)
    carries = np.ones((2, NH, NBLK // 2, 2, TPB), np.float32)
    carries[0, :, :, 0, 0] = carries[1, :, :, 1, TPB - 1] = 0
    a["carries"] = carries.reshape(-1, TPB)
    a["conv_w"] = c(np.stack(both["conv_w"]).reshape(2, 4, P, NCONV).transpose(2, 0, 1, 3))
    a["conv_b"] = c(np.stack(both["conv_b"]).reshape(2, 4, P).transpose(2, 0, 1))
    a["skip"] = c(np.repeat(np.stack(both["D"]), HD, axis=1).reshape(2, 2, P).transpose(2, 0, 1))
    a["norm_w"] = c(np.stack(both["norm_w"]).reshape(2, 2, P).transpose(2, 0, 1))
    a["w_out"] = c(np.stack([w.T for w in both["Wo"]]).reshape(2, 2, P, DM).transpose(2, 0, 1, 3))
    return a


def kernel(**inputs):
    import concourse.bacc as _bacc
    from concourse.bass_utils import run_bass_kernel_spmd as _run

    nc = _bacc.Bacc("TRN2", target_bir_lowering=False, num_devices=1)
    arrays, ins = {}, {}
    for name, a in kernel_inputs(inputs).items():
        a = np.ascontiguousarray(a)
        arrays[f"in_{name}_dram"] = a
        ins[name] = nc.dram_tensor(f"in_{name}_dram", a.shape, mybir.dt.from_np(a.dtype), kind="ExternalInput").ap()
    out = nc.dram_tensor("out_0_dram", (BATCH, SEQ, DM), F32, kind="ExternalOutput").ap()
    build(nc, ins, {"out": out})
    r = _run(nc, [arrays], core_ids=[0])
    return r.results[0]["out_0_dram"]
```
